# Optimizing a Trainium2 kernel written in Bass

```python
import numpy as np
import jax
import jax.numpy as jnp

def _softmax(x, axis=-1):
    return jax.nn.softmax(x, axis=axis)

def _gelu(x):
    return jax.nn.gelu(x, approximate=True)

def _silu(x):
    return jax.nn.silu(x)

def _sigmoid(x):
    return jax.nn.sigmoid(x)

def _layernorm(x, axis=-1, eps=1e-05):
    m = jnp.mean(x, axis=axis, keepdims=True)
    v = jnp.var(x, axis=axis, keepdims=True)
    return (x - m) / jnp.sqrt(v + eps)

def _scatter_add(tgt, idx, src, axis=0):
    return tgt.at[idx].add(src)

def _segment_sum(src, seg, n):
    return jax.ops.segment_sum(src, seg, n)
kernel_name = 'mk_decoder_preln_d1_seqx_r8_b1c0e4'

def setup_inputs(seed: int=0):
    np.random.seed(seed)
    _w = jnp.asarray

    def _rec_inputs():
        import jax
        import jax.numpy as jnp
        _rk = jax.random.key(seed)
        x = 7.22e-05 + 1 * jax.random.normal(jax.random.fold_in(_rk, 1), (16, 128, 256), jnp.float32)
        _lenS = 128 - jax.random.randint(jax.random.fold_in(_rk, 7), (16,), 0, max(1, 128 // 4) + 1, jnp.int32)
        _lenS2 = 128 - jax.random.randint(jax.random.fold_in(_rk, 8), (16,), 0, max(1, 128 // 4) + 1, jnp.int32)
        _ctx_2048P = jax.random.normal(jax.random.fold_in(_rk, 11), (16, 16, 256), jnp.float32)
        _ctx_2048c = jax.random.dirichlet(jax.random.fold_in(_rk, 511), 0.3 * jnp.ones((16,), jnp.float32), (16, 128))
        _ctx_2048t = jnp.einsum('bsk,bkd->bsd', _ctx_2048c, _ctx_2048P)
        _ctx_2048t = _ctx_2048t * jax.lax.rsqrt(jnp.mean(jnp.square(_ctx_2048t)) + 1e-12) * 0.953939
        ctx_2048 = 4.13588e-05 + 0.999923 * (_ctx_2048t + 0.3 * jax.random.normal(jax.random.fold_in(_rk, 611), (16, 128, 256), jnp.float32))
        return (x, ctx_2048)
    x, ctx_2048 = _rec_inputs()

    def _L0_attn_setup():
        import jax, jax.numpy as jnp
        import numpy as np
        D_MODEL = 256
        N_HEADS = 16
        D_HEAD = D_MODEL // N_HEADS
        WINDOW = 64
        SCALE = D_HEAD ** (-0.5)
        key = jax.random.key(seed)
        ks = jax.random.split(key, 5)
        B, S = (2, 512)
        x = jax.random.normal(ks[0], (B, S, D_MODEL), dtype=jnp.float32)
        W_qkv = jax.random.normal(ks[1], (D_MODEL, 3 * D_MODEL), dtype=jnp.float32) * D_MODEL ** (-0.5)
        b_qkv = jax.random.normal(ks[2], (3 * D_MODEL,), dtype=jnp.float32) * 0.02
        W_out = jax.random.normal(ks[3], (D_MODEL, D_MODEL), dtype=jnp.float32) * D_MODEL ** (-0.5)
        b_out = jax.random.normal(ks[4], (D_MODEL,), dtype=jnp.float32) * 0.02
        return {'x': x, 'W_qkv': W_qkv, 'b_qkv': b_qkv, 'W_out': W_out, 'b_out': b_out}
    _L0_attn_all = _L0_attn_setup()
    _L0_attn_in = {k: v for k, v in _L0_attn_all.items() if k in ('W_qkv', 'b_qkv', 'W_out', 'b_out')}
    del _L0_attn_all

    def _L0_xattn_setup():
        import jax, jax.numpy as jnp
        import numpy as np
        B, S, DIM, HD = (4, 128, 256, 128)
        H = DIM // HD
        GN_EPS = 0.001

        def _decay_masks(n_heads, seq_len):
            gam = 1.0 - 2.0 ** (-5.0 - jnp.arange(n_heads, dtype=jnp.float32))
            idx = jnp.arange(seq_len, dtype=jnp.float32)
            expo = idx[None, :] - idx[:, None]
            D = jnp.where(expo[None, :, :] <= 0, gam[:, None, None] ** expo[None, :, :], 0.0)
            return D / jnp.sqrt(D.sum(axis=-1))[:, None, :]
        key = jax.random.key(seed)
        ks = jax.random.split(key, 8)
        x = jax.random.normal(ks[0], (B, S, DIM), dtype=jnp.float32)
        k = jax.random.normal(ks[1], (B, S, DIM), dtype=jnp.float32)
        v = jax.random.normal(ks[2], (B, S, DIM), dtype=jnp.float32)
        Wh = jax.random.normal(ks[3], (H, HD, HD), dtype=jnp.float32) / np.sqrt(HD)
        wg_w = jax.random.normal(ks[4], (DIM, DIM), dtype=jnp.float32) / np.sqrt(DIM)
        wo_w = jax.random.normal(ks[5], (DIM, DIM), dtype=jnp.float32) / np.sqrt(DIM)
        gn_gamma = jnp.ones((DIM,), dtype=jnp.float32)
        gn_beta = jnp.zeros((DIM,), dtype=jnp.float32)
        return {'x': x, 'k': k, 'v': v, 'Wh': Wh, 'wg_w': wg_w, 'wo_w': wo_w, 'gn_gamma': gn_gamma, 'gn_beta': gn_beta}
    _L0_xattn_all = _L0_xattn_setup()
    _L0_xattn_in = {k: v for k, v in _L0_xattn_all.items() if k in ('Wh', 'wg_w', 'wo_w', 'gn_gamma', 'gn_beta')}
    del _L0_xattn_all

    def _L0_ffn_setup():
        import jax, jax.numpy as jnp
        import numpy as np
        DIM = 256
        N_EXPERTS = 8
        TOP_K = 2
        key = jax.random.key(seed)
        ks = jax.random.split(key, 5)
        x = jax.random.normal(ks[0], (4, 512, DIM), dtype=jnp.float32)
        W_up = jax.random.normal(ks[1], (DIM, DIM), dtype=jnp.float32) * (1.0 / np.sqrt(DIM))
        W_down = jax.random.normal(ks[2], (DIM, DIM), dtype=jnp.float32) * (1.0 / np.sqrt(DIM))
        W_gate = jax.random.normal(ks[3], (N_EXPERTS, DIM), dtype=jnp.float32) * (1.0 / np.sqrt(DIM))
        W_expert = jax.random.normal(ks[4], (DIM, DIM), dtype=jnp.float32) * (1.0 / np.sqrt(DIM))
        return {'x': x, 'W_up': W_up, 'W_down': W_down, 'W_gate': W_gate, 'W_expert': W_expert}
    _L0_ffn_all = _L0_ffn_setup()
    _L0_ffn_in = {k: v for k, v in _L0_ffn_all.items() if k in ('W_up', 'W_down', 'W_gate', 'W_expert')}
    del _L0_ffn_all
    return {'x': x, 'ctx_2048': ctx_2048, 'L0_attn_W_qkv': _L0_attn_in['W_qkv'], 'L0_attn_b_qkv': _L0_attn_in['b_qkv'], 'L0_attn_W_out': _L0_attn_in['W_out'], 'L0_attn_b_out': _L0_attn_in['b_out'], 'L0_xattn_Wh': _L0_xattn_in['Wh'], 'L0_xattn_wg_w': _L0_xattn_in['wg_w'], 'L0_xattn_wo_w': _L0_xattn_in['wo_w'], 'L0_xattn_gn_gamma': _L0_xattn_in['gn_gamma'], 'L0_xattn_gn_beta': _L0_xattn_in['gn_beta'], 'L0_ffn_W_up': _L0_ffn_in['W_up'], 'L0_ffn_W_down': _L0_ffn_in['W_down'], 'L0_ffn_W_gate': _L0_ffn_in['W_gate'], 'L0_ffn_W_expert': _L0_ffn_in['W_expert']}

def reference(x, ctx_2048, L0_attn_W_qkv, L0_attn_b_qkv, L0_attn_W_out, L0_attn_b_out, L0_xattn_Wh, L0_xattn_wg_w, L0_xattn_wo_w, L0_xattn_gn_gamma, L0_xattn_gn_beta, L0_ffn_W_up, L0_ffn_W_down, L0_ffn_W_gate, L0_ffn_W_expert):
    import jax
    import jax.numpy as jnp

    def _L0_attn_ref(x, W_qkv, b_qkv, W_out, b_out):
        import jax, jax.numpy as jnp
        import numpy as np
        D_MODEL = 256
        N_HEADS = 16
        D_HEAD = D_MODEL // N_HEADS
        WINDOW = 64
        SCALE = D_HEAD ** (-0.5)
        B, S, D = x.shape
        nb = S // WINDOW
        qkv = x @ W_qkv + b_qkv
        q, k, v = jnp.split(qkv, 3, axis=-1)

        def to_blocks(t):
            return t.reshape(B, nb, WINDOW, N_HEADS, D_HEAD).transpose(0, 3, 1, 2, 4)
        q, k, v = (to_blocks(q), to_blocks(k), to_blocks(v))
        scores = jnp.einsum('bhnqd,bhnkd->bhnqk', q, k) * SCALE
        causal = jnp.tril(jnp.ones((WINDOW, WINDOW), dtype=bool))
        scores = jnp.where(causal, scores, -jnp.inf)
        attn = jax.nn.softmax(scores, axis=-1)
        out = jnp.einsum('bhnqk,bhnkd->bhnqd', attn, v)
        out = out.transpose(0, 2, 3, 1, 4).reshape(B, S, D)
        return out @ W_out + b_out

    def _L0_xattn_ref(x, k, v, Wh, wg_w, wo_w, gn_gamma, gn_beta):
        import jax, jax.numpy as jnp
        import numpy as np
        B, S, DIM, HD = (4, 128, 256, 128)
        H = DIM // HD
        GN_EPS = 0.001

        def _decay_masks(n_heads, seq_len):
            gam = 1.0 - 2.0 ** (-5.0 - jnp.arange(n_heads, dtype=jnp.float32))
            idx = jnp.arange(seq_len, dtype=jnp.float32)
            expo = idx[None, :] - idx[:, None]
            D = jnp.where(expo[None, :, :] <= 0, gam[:, None, None] ** expo[None, :, :], 0.0)
            return D / jnp.sqrt(D.sum(axis=-1))[:, None, :]
        b, s, dim = x.shape
        h, hd, _ = Wh.shape
        xh = x.reshape(b, s, h, hd)
        kh = k.reshape(b, s, h, hd)
        vh = v.reshape(b, s, h, hd)
        Q = jnp.einsum('bshd,hde->bshe', xh, Wh)
        K = jnp.einsum('bshd,hde->bshe', kh, Wh)
        V = jnp.einsum('bshd,hde->bshe', vh, Wh)
        scores = jnp.einsum('bshe,bthe->bhst', Q, K) / jnp.sqrt(jnp.float32(hd))
        Dn = _decay_masks(h, s)
        masked = scores * Dn[None, :, :, :]
        A = jnp.maximum(jnp.abs(masked.sum(axis=0)), 1.0)
        O = jnp.einsum('hst,bthe->bshe', A, V).reshape(b, s, dim)
        mu = O.mean(axis=-1, keepdims=True)
        var = O.var(axis=-1, keepdims=True)
        Y = (O - mu) / jnp.sqrt(var + GN_EPS) * gn_gamma + gn_beta
        W = jax.nn.relu(x @ wg_w)
        return W * Y @ wo_w

    def _L0_ffn_ref(x, W_up, W_down, W_gate, W_expert):
        import jax, jax.numpy as jnp
        import numpy as np
        DIM = 256
        N_EXPERTS = 8
        TOP_K = 2
        logits = jnp.einsum('bsd,ed->bse', x, W_gate)
        routing_weights, selected_experts = jax.lax.top_k(logits, TOP_K)
        shared_out = jnp.einsum('bsd,od->bso', jax.nn.relu(jnp.einsum('bsd,od->bso', x, W_up)), W_down)
        rw = jax.nn.softmax(routing_weights, axis=-1)
        expert_out = jnp.einsum('bsd,do->bso', x, W_expert)
        moe_out = jnp.sum(rw, axis=-1, keepdims=True) * expert_out
        return shared_out + moe_out
    x = x + _L0_attn_ref(_layernorm(x, axis=-1), L0_attn_W_qkv, L0_attn_b_qkv, L0_attn_W_out, L0_attn_b_out)
    x = x + _L0_xattn_ref(_layernorm(x, axis=-1), ctx_2048, ctx_2048, L0_xattn_Wh, L0_xattn_wg_w, L0_xattn_wo_w, L0_xattn_gn_gamma, L0_xattn_gn_beta)
    x = x + _L0_ffn_ref(_layernorm(x, axis=-1), L0_ffn_W_up, L0_ffn_W_down, L0_ffn_W_gate, L0_ffn_W_expert)
    return x

_drawn_inputs = setup_inputs


def setup_inputs(seed=0):
    import zlib

    import numpy as np

    out = dict(_drawn_inputs(seed))
    spreads = {'L0_xattn_gn_gamma': (1.0, 0.2), 'L0_xattn_gn_beta': (0.0, 0.1)}
    factors = {'L0_attn_b_out': 3.044, 'L0_ffn_W_gate': 8.0}
    for name, (base, spread) in spreads.items():
        noise = np.random.default_rng([zlib.crc32(name.encode()), seed]).standard_normal(out[name].shape)
        drawn = base * np.exp(spread * noise) if base else spread * noise
        out[name] = jnp.asarray(drawn.astype(out[name].dtype))
    for name, factor in factors.items():
        out[name] = (out[name] * factor).astype(out[name].dtype)
    return out
```

```python
from contextlib import ExitStack

import concourse.bass as bass
from concourse import mybir

ALU = mybir.AluOpType
ACT = mybir.ActivationFunctionType
F32 = mybir.dt.float32
BF16 = mybir.dt.bfloat16
AX_X = mybir.AxisListType.X

P = 128
LN_EPS = 1e-5
GN_EPS = 1e-3
WINDOW = 64
HEADS = 16
DH = 16
ATT_SCALE = float(DH) ** -0.5


def bass_decoder_layer_kernel(nc, x, ctx_in, w_qkv, b_qk, b_v, w_out, b_out, wh, wg, wo, gamma, beta,
                              w_up, w_down, w_gate, w_expert, ident_in, mask_sel_in, mask_in, decay_in, out):
    B, S, D = x.shape
    KT = D // P
    TPC = 2
    NC = B // TPC
    TOK = TPC * P
    NW = S // WINDOW
    HPH = HEADS // KT
    PAIRS = HEADS // 2
    VW = DH + 1
    E = w_gate.shape[0]
    assert S == P and D == 2 * P and NW == 2

    with ExitStack() as ctx:
        def sb(name, shape, dt=F32):
            return ctx.enter_context(nc.sbuf_tensor(name, shape, dt))

        def pb(name):
            return ctx.enter_context(nc.psum_tensor(name, [P, 512], F32))

        def sem(name):
            return ctx.enter_context(nc.semaphore(name))

        x_all = sb("x_all", [P, NC, TPC * D])
        v_all = sb("v_all", [P, KT, NC, TOK])
        wT_all = sb("wT_all", [P, KT, NC, TOK])
        wqkv_sb = sb("wqkv_sb", [P, KT, 3 * D])
        wout_sb = sb("wout_sb", [P, KT, D])
        wh_sb = sb("wh_sb", [P, KT, P])
        whT_sb = sb("whT_sb", [P, KT, P])
        gram_sb = sb("gram_sb", [P, KT, P])
        wg_sb = sb("wg_sb", [P, KT, D])
        wo_sb = sb("wo_sb", [P, KT, D])
        wup_sb = sb("wup_sb", [P, KT, D])
        wdn_sb = sb("wdn_sb", [P, KT, D])
        wgate_sb = sb("wgate_sb", [E, D])
        wupT_sb = sb("wupT_sb", [P, KT, D])
        wdnT_sb = sb("wdnT_sb", [P, KT, D])
        wex_sb = sb("wex_sb", [P, KT, D + E])
        bqk_sb = sb("bqk_sb", [P, 2 * KT])
        bv_sb = sb("bv_sb", [P, D])
        bout_sb = sb("bout_sb", [P, D])
        gb_sb = sb("gb_sb", [P, 2 * KT])
        ident = sb("ident", [P, P])
        mask_sel = sb("mask_sel", [P, P], BF16)
        mask = sb("mask", [P, WINDOW], BF16)
        decay = sb("decay", [P, KT, P])
        zeros = sb("zeros", [P, 2 * P], BF16)
        minus_half, ln_eps, gn_eps = (sb(n, [P, TPC]) for n in ("minus_half", "ln_eps", "gn_eps"))
        hn = sb("hn", [P, TPC, D])
        ctx_sb = sb("ctx_sb", [P, TPC, D])
        hT = sb("hT", [P, KT, TOK])
        kT = sb("kT", [P, KT, TOK])
        qT = sb("qT", [P, KT, TOK])
        k_heads = sb("k_heads", [P, KT, HPH, TOK])
        v_pairs = sb("v_pairs", [P, TPC, NW, PAIRS, 2, VW])
        probs = [sb(f"probs{n}", [P, HPH, WINDOW]) for n in range(2)]
        probsT = [sb(f"probsT{n}", [P, 512]) for n in range(2)]
        rowmax = sb("rowmax", [P, 2, HPH])
        rsum = sb("rsum", [P, TPC, HEADS])
        att = sb("att", [P, TPC, D])
        attT = sb("attT", [P, KT, TOK])
        x1n = sb("x1n", [P, TPC, D])
        x1nT = sb("x1nT", [P, KT, TOK])
        qpT = sb("qpT", [P, KT, TOK])
        ctxT = sb("ctxT", [P, KT, TOK])
        bn1, bn2, bn3, bn4 = (sb(f"bn{n}", [P, TPC, 6]) for n in range(1, 5))
        mv1, mv2, mv3, mv4 = (sb(f"mv{n}", [P, TPC, 2]) for n in range(1, 5))
        ve1, ve2, ve3, ve4 = (sb(f"ve{n}", [P, TPC]) for n in range(1, 5))
        rs1, rs2, rs3, rs4 = (sb(f"rs{n}", [P, TPC]) for n in range(1, 5))
        dec = sb("dec", [P, KT * P])
        dabs = sb("dabs", [P, KT * P])
        aT = sb("aT", [P, KT, P])
        on = sb("on", [P, TPC, D])
        yT = sb("yT", [P, KT, TOK])
        zT = sb("zT", [P, KT, TOK])
        x2n = sb("x2n", [P, TPC, D])
        x2nT = sb("x2nT", [P, KT, TOK])
        uT = sb("uT", [P, KT, TOK])
        top = sb("top", [P, TPC, 8])
        ldiff = sb("ldiff", [P, TPC])
        esec = sb("esec", [P, TPC])
        eden = sb("eden", [P, TPC])
        einv = sb("einv", [P, TPC])
        rw = sb("rw", [P, TPC])

        s_bank = [pb("s_bank0"), pb("s_bank1")]
        t_bank = [pb("t_bank0"), pb("t_bank1")]
        o_bank = pb("o_bank")
        g_bank = [pb("g_bank0"), pb("g_bank1")]
        c_bank = pb("c_bank")

        ld_x0, ld_x, ld_ctx, ld_wqkv, ld_const, ld_w = map(
            sem, "ld_x0 ld_x ld_ctx ld_wqkv ld_const ld_w".split())
        pool_const = sem("pool_const")
        turned, turned_out = sem("turned"), sem("turned_out")
        hT_ps, k_ps, q_ps, v_ps, attT_ps, y_ps = map(sem, "hT_ps k_ps q_ps v_ps attT_ps y_ps".split())
        x1nT_ps, w_ps, qp_ps, ctxT_ps, vx_ps, sc_ps = map(sem, "x1nT_ps w_ps qp_ps ctxT_ps vx_ps sc_ps".split())
        s_ps, pT_ps, pv_ps = map(sem, "s_ps pT_ps pv_ps".split())
        hT_sb, k_sb, q_sb, v_sb, attT_sb, x1_sb = map(sem, "hT_sb k_sb q_sb v_sb attT_sb x1_sb".split())
        x1nT_sb, w_sb, qp_sb, ctxT_sb, vx_sb = map(sem, "x1nT_sb w_sb qp_sb ctxT_sb vx_sb".split())
        max_sb, sub_sb, exp_sb, pT_sb, rsum_sb, att_sb = map(sem, "max_sb sub_sb exp_sb pT_sb rsum_sb att_sb".split())
        kh_dma = sem("kh_dma")
        st1, ag1, pe1, ps1, hn_sb, xb_sb = map(sem, "st1 ag1 pe1 ps1 hn_sb xb_sb".split())
        st2, ag2, pe2, ps2, x1n_sb = map(sem, "st2 ag2 pe2 ps2 x1n_sb".split())
        st3, ag3, pe3, ps3, on_sb = map(sem, "st3 ag3 pe3 ps3 on_sb".split())
        st4, ag4, pe4, ps4, x2n_sb = map(sem, "st4 ag4 pe4 ps4 x2n_sb".split())
        dec_sb, abs_sb, aT_sb = map(sem, "dec_sb abs_sb aT_sb".split())
        o_ps, yT_ps, z_ps, x2nT_ps, up_ps, ex_ps, dn_ps = map(sem, "o_ps yT_ps z_ps x2nT_ps up_ps ex_ps dn_ps".split())
        yT_sb, zT_sb, x2_sb, x2nT_sb, uT_sb = map(sem, "yT_sb zT_sb x2_sb x2nT_sb uT_sb".split())
        top_sb, ld_sb, es_sb, ed_sb, ei_sb, rw_sb, acc_sb, out_sb = map(
            sem, "top_sb ld_sb es_sb ed_sb ei_sb rw_sb acc_sb out_sb".split())
        st_out = sem("st_out")

        x_dram = x.rearrange("(c t) s d -> s c t d", t=TPC)
        ctx_dram = ctx_in.rearrange("(c t) s d -> s c t d", t=TPC)
        out_dram = out.rearrange("(c t) s d -> s c t d", t=TPC)

        def tiles(ap):
            return ap.rearrange("p (t d) -> p t d", t=TPC)

        def halves(bank, n=512):
            return bank[:, 0:n].rearrange("p (k n) -> p k n", k=KT)

        def split(w):
            return w.rearrange("(k p) n -> p k n", p=P)

        UNITS = TPC * KT
        NK = HPH
        LOADS_CONST = 6
        LOADS_W = 11

        block = ctx.enter_context(nc.Block())

        @block.sync
        def _(sp):
            sp.dma_start(tiles(x_all[:, 0, :]), x_dram[:, 0]).then_inc(ld_x0, 16)
            sp.dma_start(x_all[:, 1:NC, :].rearrange("p c (t d) -> p c t d", t=TPC), x_dram[:, 1:NC]).then_inc(ld_x, 16)
            sp.dma_start(ctx_sb[:, :, :], ctx_dram[:, 0]).then_inc(ld_ctx, 16)

            def spread_keys(c):
                sp.wait_ge(k_sb, c + 1)
                for h in range(HPH):
                    rows = slice(DH * h, DH * h + DH)
                    sp.dma_start(k_heads[rows, :, h, :], kT[rows, :, :]).then_inc(kh_dma, 16)

            sp.wait_ge(pool_const, 1)
            spread_keys(0)
            with sp.Fori(1, NC) as c:
                spread_keys(c)
                sp.wait_ge(ctxT_ps, c)
                sp.dma_start(ctx_sb[:, :, :], ctx_dram[:, c]).then_inc(ld_ctx, 16)
            with sp.Fori(0, NC) as c:
                sp.wait_ge(out_sb, TPC * (c + 1))
                sp.dma_start(out_dram[:, c], tiles(x_all[:, c, :])).then_inc(st_out, 16)
            sp.wait_ge(st_out, 16 * NC)

        @block.gpsimd
        def _(pool):
            pool.memset(minus_half[:, :], -0.5)
            pool.memset(ln_eps[:, :], LN_EPS)
            pool.memset(gn_eps[:, :], GN_EPS)
            pool.memset(zeros[:, :], 0.0)
            pool.memset(k_heads[:, :, :, :], 0.0).then_inc(pool_const, 1)
            pool.memset(v_pairs[:, :, :, :, :, :], 0.0).then_inc(pool_const, 1)
            pool.wait_ge(pool_const, 2)
            for h in range(2):
                rows = slice(WINDOW * h, WINDOW * h + WINDOW)
                pool.memset(v_pairs[rows, :, :, :, h, DH:VW], 1.0).then_inc(pool_const, 1)
                pool.wait_ge(pool_const, 3 + h)

            def rsqrt(c, mv, ve, rs, ag, pe, ps, eps):
                pool.wait_ge(ag, TPC * (c + 1))
                pool.tensor_tensor(ve[:, :], mv[:, :, 1], eps[:, :], ALU.add).then_inc(pe, 1)
                pool.wait_ge(pe, c + 1)
                pool.tensor_tensor(rs[:, :], ve[:, :], minus_half[:, :], ALU.pow).then_inc(ps, 1)

            def add_bias(c):
                pool.wait_ge(hn_sb, TPC * (c + 1))
                for t in range(TPC):
                    xt = x_all[:, c, t * D:(t + 1) * D]
                    pool.tensor_tensor(xt, xt, bout_sb[:, :], ALU.add).then_inc(xb_sb, 1)

            rsqrt(0, mv1, ve1, rs1, ag1, pe1, ps1, ln_eps)
            pool.wait_ge(ld_w, LOADS_W * 16)
            add_bias(0)
            with pool.Fori(0, NC - 1) as i:
                rsqrt(i + 1, mv1, ve1, rs1, ag1, pe1, ps1, ln_eps)
                add_bias(i + 1)
                rsqrt(i, mv2, ve2, rs2, ag2, pe2, ps2, ln_eps)
            rsqrt(NC - 1, mv2, ve2, rs2, ag2, pe2, ps2, ln_eps)
            rsqrt(0, mv3, ve3, rs3, ag3, pe3, ps3, gn_eps)
            with pool.Fori(1, NC) as c:
                rsqrt(c, mv3, ve3, rs3, ag3, pe3, ps3, gn_eps)
                rsqrt(c - 1, mv4, ve4, rs4, ag4, pe4, ps4, ln_eps)
            rsqrt(NC - 1, mv4, ve4, rs4, ag4, pe4, ps4, ln_eps)

        @block.scalar
        def _(act):
            act.dma_start(ident[:, :], ident_in).then_inc(ld_const, 16)
            act.dma_start(wqkv_sb[:, :, :], split(w_qkv)).then_inc(ld_wqkv, 16)
            act.dma_start(bqk_sb[:, :], b_qk).then_inc(ld_const, 16)
            act.dma_start(bv_sb[:, :], b_v).then_inc(ld_const, 16)
            act.dma_start(mask_sel[:, :], mask_sel_in).then_inc(ld_const, 16)
            act.dma_start(mask[:, :], mask_in).then_inc(ld_const, 16)
            act.dma_start(decay[:, :, :], decay_in).then_inc(ld_const, 16)
            act.dma_start(gb_sb[:, 0:KT], gamma).then_inc(ld_w, 16)
            act.dma_start(wh_sb[:, :, :], wh.rearrange("h d e -> d h e")).then_inc(ld_w, 16)
            act.dma_start(wup_sb[:, :, :], split(w_up)).then_inc(ld_w, 16)
            act.dma_start(wdn_sb[:, :, :], split(w_down)).then_inc(ld_w, 16)
            act.dma_start(wgate_sb[:, :], w_gate).then_inc(ld_w, 16)
            act.dma_start(wout_sb[:, :, :], split(w_out)).then_inc(ld_w, 16)
            act.dma_start(bout_sb[:, :], b_out).then_inc(ld_w, 16)
            act.dma_start(wg_sb[:, :, :], split(wg)).then_inc(ld_w, 16)
            act.dma_start(wo_sb[:, :, :], split(wo)).then_inc(ld_w, 16)
            act.dma_start(wex_sb[:, :, 0:D], split(w_expert)).then_inc(ld_w, 16)
            act.dma_start(gb_sb[:, KT:2 * KT], beta).then_inc(ld_w, 16)

            def hT_out(c):
                act.wait_ge(hT_ps, c + 1)
                act.activation(hT[:, :, :], halves(g_bank[0]), ACT.Copy).then_inc(hT_sb, 1)

            def k_out(c, bank):
                act.wait_ge(k_ps, c + 1)
                for k in range(KT):
                    last = act.activation(kT[:, k, :], halves(bank)[:, k, :], ACT.Identity,
                                          bias=bqk_sb[:, KT + k:KT + k + 1])
                last.then_inc(k_sb, 1)

            def q_out(c, bank):
                act.wait_ge(q_ps, c + 1)
                for k in range(KT):
                    last = act.activation(qT[:, k, :], halves(bank)[:, k, :], ACT.Identity,
                                          bias=bqk_sb[:, k:k + 1])
                last.then_inc(q_sb, 1)

            def exps(i, u):
                act.wait_ge(sub_sb, UNITS * i + u + 1)
                p = probs[u % 2]
                act.activation(p[:, :, :], p[:, :, :], ACT.Exp, scale=ATT_SCALE).then_inc(exp_sb, 1)

            def probsT_out(i, u):
                act.wait_ge(pT_ps, UNITS * i + u + 1)
                act.activation(probsT[u % 2][:, :], t_bank[u % 2][:, :], ACT.Copy).then_inc(pT_sb, 1)

            def attention(i, first, last):
                exps(i, 0)
                if not first:
                    act.wait_ge(x1nT_ps, i)
                    act.activation(x1nT[:, :, :], halves(g_bank[1]), ACT.Copy).then_inc(x1nT_sb, 1)
                exps(i, 1)
                probsT_out(i, 0)
                exps(i, 2)
                probsT_out(i, 1)
                exps(i, 3)
                if not first:
                    act.wait_ge(w_ps, i)
                    act.activation(wT_all[:, :, i - 1, :], halves(g_bank[0]), ACT.Relu).then_inc(w_sb, 1)
                probsT_out(i, 2)
                if not first:
                    act.wait_ge(qp_ps, i)
                    act.activation(qpT[:, :, :], halves(g_bank[1]), ACT.Copy).then_inc(qp_sb, 1)
                probsT_out(i, 3)
                if not last:
                    hT_out(i + 1)
                act.wait_ge(ctxT_ps, i + 1)
                act.activation(ctxT[:, :, :], halves(g_bank[1]), ACT.Copy).then_inc(ctxT_sb, 1)
                if not last:
                    k_out(i + 1, g_bank[0])
                    q_out(i + 1, g_bank[1])
                act.wait_ge(attT_ps, i + 1)
                act.activation(attT[:, :, :], halves(g_bank[1]), ACT.Copy).then_inc(attT_sb, 1)
                act.wait_ge(vx_ps, i + 1)
                act.activation(v_all[:, :, i, :], halves(g_bank[1]), ACT.Copy).then_inc(vx_sb, 1)

            act.wait_ge(ld_const, 16 * LOADS_CONST)
            hT_out(0)
            k_out(0, g_bank[1])
            q_out(0, g_bank[0])
            for n, (dst, src) in enumerate((
                    (whT_sb[:, :, :], halves(g_bank[0], KT * P)),
                    (wupT_sb[:, :, :], halves(g_bank[1])),
                    (wdnT_sb[:, :, :], halves(g_bank[0])),
                    (wex_sb[:, :, D:D + E], halves(g_bank[1], KT * E)),
                    (gram_sb[:, :, :], halves(g_bank[0], KT * P)))):
                act.wait_ge(turned, n + 1)
                act.activation(dst, src, ACT.Copy).then_inc(turned_out, 1)

            attention(0, True, False)
            with act.Fori(1, NC - 1) as i:
                attention(i, False, False)
            attention(NC - 1, False, True)
            act.wait_ge(x1nT_ps, NC)
            act.activation(x1nT[:, :, :], halves(g_bank[1]), ACT.Copy).then_inc(x1nT_sb, 1)
            act.wait_ge(w_ps, NC)
            act.activation(wT_all[:, :, NC - 1, :], halves(g_bank[0]), ACT.Relu).then_inc(w_sb, 1)
            act.wait_ge(qp_ps, NC)
            act.activation(qpT[:, :, :], halves(g_bank[1]), ACT.Copy).then_inc(qp_sb, 1)

            act.wait_ge(ld_w, 16 * LOADS_W)

            def y_out(c):
                act.wait_ge(yT_ps, c + 1)
                for k in range(KT):
                    act.activation(yT[:, k, :], halves(t_bank[0])[:, k, :], ACT.Identity,
                                   scale=gb_sb[:, k:k + 1], bias=gb_sb[:, KT + k:KT + k + 1]).then_inc(yT_sb, 1)

            def second(c, head, tail):
                if head:
                    act.wait_ge(x2nT_ps, c)
                    act.activation(x2nT[:, :, :], halves(t_bank[1]), ACT.Copy).then_inc(x2nT_sb, 1)
                if tail:
                    y_out(c)
                if head:
                    act.wait_ge(up_ps, c)
                    act.activation(uT[:, :, :], halves(s_bank[0]), ACT.Relu).then_inc(uT_sb, 1)
                    act.wait_ge(ld_sb, c)
                    act.activation(esec[:, :], ldiff[:, :], ACT.Exp).then_inc(es_sb, 1)

            second(0, False, True)
            with act.Fori(1, NC) as c:
                second(c, True, True)
            second(NC, True, False)

        @block.vector
        def _(dve):
            def norm_stats(c, src, bn, mv, st, ag, source=None):
                dve.wait_ge(ld_x0, 16)
                if source is not None:
                    dve.wait_ge(source, c + 1)
                for t in range(TPC):
                    dve.bn_stats(bn[:, t, :], src(t)).then_inc(st, 1)
                dve.drain()
                for t in range(TPC):
                    dve.bn_aggr(mv[:, t, :], bn[:, t, :]).then_inc(ag, 1)

            def normalize(c, src, dst, mv, rs, ps, done):
                dve.wait_ge(ps, c + 1)
                for t in range(TPC):
                    dve.tensor_scalar(dst[:, t, :], src(t), mv[:, t, 0:1], rs[:, t:t + 1],
                                      ALU.subtract, ALU.mult).then_inc(done, 1)

            def x_tile(c):
                return lambda t: x_all[:, c, t * D:(t + 1) * D]

            def o_tile(t):
                return o_bank[:, t * D:(t + 1) * D]

            def soften(i, u, started):
                bank = s_bank[u % 2][:, :].rearrange("p (h k) -> p h k", h=HPH)
                dve.wait_ge(s_ps, UNITS * i + u + 1)
                dve.tensor_reduce(rowmax[:, u % 2, :], bank, AX_X, ALU.max).then_inc(max_sb, 1)
                dve.wait_ge(max_sb, UNITS * i + u + 1)
                if started or u >= 2:
                    dve.wait_ge(pT_ps, UNITS * i + u - 1)
                dve.tensor_tensor(probs[u % 2][:, :, :], bank,
                                  rowmax[:, u % 2, :].unsqueeze(2).broadcast_to([P, HPH, WINDOW]),
                                  ALU.subtract).then_inc(sub_sb, 1)

            def v_out(c, bank):
                dve.wait_ge(v_ps, c + 1)
                src = bank[:, :].rearrange("p (t j h d) -> p t j h d", t=TPC, h=2, d=DH)
                bias = bv_sb[:, :].rearrange("p (j h d) -> p j h d", h=2, d=DH)
                for w in range(NW):
                    for h in range(2):
                        wr = slice(WINDOW * w, WINDOW * w + WINDOW)
                        hr = slice(WINDOW * h, WINDOW * h + WINDOW)
                        last = dve.tensor_tensor(
                            v_pairs[hr, :, w, :, h, 0:DH], src[wr, :, :, h, :],
                            bias[wr, :, h, :].unsqueeze(1).broadcast_to([WINDOW, TPC, PAIRS, DH]), ALU.add)
                last.then_inc(v_sb, 1)

            def att_out(i, t):
                o = o_bank[:, 0:HEADS * VW].rearrange("p (h v) -> p h v", v=VW)
                dve.wait_ge(pv_ps, UNITS * i + KT * (t + 1))
                dve.reciprocal(rsum[:, t, :], o[:, :, DH]).then_inc(rsum_sb, 1)
                dve.wait_ge(rsum_sb, TPC * i + t + 1)
                dve.tensor_tensor(att[:, t, :].rearrange("p (h d) -> p h d", d=DH), o[:, :, 0:DH],
                                  rsum[:, t, :].unsqueeze(2).broadcast_to([P, HEADS, DH]),
                                  ALU.mult).then_inc(att_sb, 1)

            def x1_out(i):
                dve.wait_ge(y_ps, i + 1)
                dve.wait_ge(xb_sb, TPC * (i + 1))
                dve.tensor_tensor(x_all[:, i, :], g_bank[0][:, :], x_all[:, i, :], ALU.add).then_inc(x1_sb, 1)
                norm_stats(i, x_tile(i), bn2, mv2, st2, ag2, x1_sb)
                normalize(i, x_tile(i), x1n, mv2, rs2, ps2, x1n_sb)

            def attention(i, started, last):
                soften(i, 0, started)
                soften(i, 1, started)
                if not last:
                    norm_stats(i + 1, x_tile(i + 1), bn1, mv1, st1, ag1)
                soften(i, 2, started)
                soften(i, 3, started)
                if not last:
                    normalize(i + 1, x_tile(i + 1), hn, mv1, rs1, ps1, hn_sb)
                att_out(i, 0)
                att_out(i, 1)
                if not last:
                    v_out(i + 1, g_bank[0])
                x1_out(i)

            dve.wait_ge(ld_x0, 16)
            norm_stats(0, x_tile(0), bn1, mv1, st1, ag1)
            normalize(0, x_tile(0), hn, mv1, rs1, ps1, hn_sb)
            dve.wait_ge(ld_const, 16 * LOADS_CONST)
            dve.wait_ge(pool_const, 4)
            v_out(0, g_bank[1])
            dve.wait_ge(ld_x, 16)
            attention(0, False, False)
            with dve.Fori(1, NC - 1) as i:
                attention(i, True, False)
            attention(NC - 1, True, True)

            dve.wait_ge(sc_ps, NC)
            dve.tensor_tensor(dec[:, :], c_bank[:, 0:KT * P], decay[:, :, :].rearrange("p k n -> p (k n)"),
                              ALU.mult).then_inc(dec_sb, 1)
            dve.wait_ge(dec_sb, 1)
            dve.scalar_tensor_tensor(out=dabs[:, :], in0=dec[:, :], scalar=-1.0, in1=dec[:, :],
                                     op0=ALU.mult, op1=ALU.max).then_inc(abs_sb, 1)
            dve.wait_ge(abs_sb, 1)
            dve.tensor_scalar(aT[:, :, :].rearrange("p k n -> p (k n)"), dabs[:, :], 1.0, None,
                              ALU.max).then_inc(aT_sb, 1)

            def o_norm(c):
                norm_stats(c, o_tile, bn3, mv3, st3, ag3, o_ps)
                normalize(c, o_tile, on, mv3, rs3, ps3, on_sb)

            def gate(c):
                dve.wait_ge(yT_sb, KT * (c + 1))
                dve.tensor_tensor(zT[:, :, :], yT[:, :, :], wT_all[:, :, c, :], ALU.mult).then_inc(zT_sb, 1)

            def x2_out(c):
                dve.wait_ge(z_ps, c + 1)
                dve.tensor_tensor(x_all[:, c, :], g_bank[1][:, :], x_all[:, c, :], ALU.add).then_inc(x2_sb, 1)
                norm_stats(c, x_tile(c), bn4, mv4, st4, ag4, x2_sb)
                normalize(c, x_tile(c), x2n, mv4, rs4, ps4, x2n_sb)

            def finish(c):
                dve.wait_ge(ld_x0, 16)
                dve.wait_ge(ex_ps, c + 1)
                for t, bank in enumerate((s_bank[1], g_bank[0])):
                    dve.max(top[:, t, :], bank[:, D:D + E]).then_inc(top_sb, 1)
                dve.wait_ge(top_sb, TPC * (c + 1))
                dve.tensor_tensor(ldiff[:, :], top[:, :, 1], top[:, :, 0], ALU.subtract).then_inc(ld_sb, 1)
                dve.wait_ge(es_sb, c + 1)
                dve.tensor_scalar(eden[:, :], esec[:, :], 1.0, None, ALU.add).then_inc(ed_sb, 1)
                dve.wait_ge(ed_sb, c + 1)
                dve.reciprocal(einv[:, :], eden[:, :]).then_inc(ei_sb, 1)
                dve.wait_ge(ei_sb, c + 1)
                for t in range(TPC):
                    last = dve.scalar_tensor_tensor(out=rw[:, t:t + 1], in0=esec[:, t:t + 1], scalar=einv[:, t:t + 1],
                                                    in1=einv[:, t:t + 1], op0=ALU.mult, op1=ALU.add)
                last.then_inc(rw_sb, 1)
                dve.wait_ge(dn_ps, c + 1)
                dve.tensor_tensor(x_all[:, c, :], c_bank[:, :], x_all[:, c, :], ALU.add).then_inc(acc_sb, 1)
                dve.wait_ge(rw_sb, c + 1)
                dve.wait_ge(acc_sb, c + 1)
                for t, bank in enumerate((s_bank[1], g_bank[0])):
                    xt = x_all[:, c, t * D:(t + 1) * D]
                    dve.scalar_tensor_tensor(out=xt, in0=bank[:, 0:D], scalar=rw[:, t:t + 1], in1=xt,
                                             op0=ALU.mult, op1=ALU.add).then_inc(out_sb, 1)

            o_norm(0)
            gate(0)
            o_norm(1)
            x2_out(0)
            with dve.Fori(1, NC - 1) as c:
                gate(c)
                o_norm(c + 1)
                x2_out(c)
                finish(c - 1)
            gate(NC - 1)
            x2_out(NC - 1)
            finish(NC - 2)
            finish(NC - 1)

        @block.tensor
        def _(pe):
            def turn(bank, src, done):
                for k in range(KT):
                    for t in range(TPC):
                        last = pe.transpose(bank[:, k * TOK + t * P:k * TOK + t * P + P], src(t, k), ident[:, :])
                last.then_inc(done, 1)

            def by_block(tile):
                return lambda t, k: tile[:, t, k * P:(k + 1) * P]

            def features(bank, w, col, srcT, done):
                for f in range(KT):
                    for k in range(KT):
                        last = pe.matmul(bank[:, f * TOK:(f + 1) * TOK], w[:, k, col + f * P:col + (f + 1) * P],
                                         srcT[:, k, :], start=(k == 0), stop=(k == KT - 1))
                last.then_inc(done, 1)

            def tokens(bank, srcT, w, col, done):
                for t in range(TPC):
                    for k in range(KT):
                        last = pe.matmul(bank[:, t * D:(t + 1) * D], srcT[:, k, t * P:(t + 1) * P],
                                         w[:, k, col:col + D], start=(k == 0), stop=(k == KT - 1))
                last.then_inc(done, 1)

            def scores(i, u, started):
                t, k = divmod(u, KT)
                bank = s_bank[u % 2]
                if started or u >= 2:
                    pe.wait_ge(sub_sb, UNITS * i + u - 1)
                if u == 0:
                    pe.wait_ge(kh_dma, 16 * NK * (i + 1))
                    pe.wait_ge(q_sb, i + 1)
                pe.matmul(bank[:, :], mask_sel[:, :], mask[:, :].unsqueeze(1).broadcast_to([P, HPH, WINDOW]),
                          start=True, stop=False, skip_group_check=True)
                for w in range(NW):
                    at = t * P + w * WINDOW
                    last = pe.matmul(bank[WINDOW * w:WINDOW * (w + 1), :], qT[:, k, at:at + WINDOW],
                                     k_heads[:, k, :, at:at + WINDOW], start=False, stop=True,
                                     skip_group_check=True)
                last.then_inc(s_ps, 1)

            def turn_probs(i, u, started):
                pe.wait_ge(exp_sb, UNITS * i + u + 1)
                if started or u >= 2:
                    pe.wait_ge(pT_sb, UNITS * i + u - 1)
                for j in range(HPH // 2):
                    src = probs[u % 2][:, 2 * j:2 * j + 2, :].rearrange("p h k -> p (h k)")
                    last = pe.transpose(t_bank[u % 2][:, j * P:(j + 1) * P], src, ident[:, :])
                last.then_inc(pT_ps, 1)

            def values(i, u, started):
                t, k = divmod(u, KT)
                pe.wait_ge(pT_sb, UNITS * i + u + 1)
                if u == 0:
                    pe.wait_ge(v_sb, i + 1)
                if k == 0 and (started or t):
                    pe.wait_ge(att_sb, TPC * i + t)
                for j in range(HPH // 2):
                    pair = k * HPH // 2 + j
                    for w in range(NW):
                        last = pe.matmul(
                            o_bank[WINDOW * w:WINDOW * (w + 1), pair * 2 * VW:(pair + 1) * 2 * VW],
                            probsT[u % 2][:, j * P + WINDOW * w:j * P + WINDOW * (w + 1)],
                            v_pairs[:, t, w, pair, :, :].rearrange("p h v -> p (h v)"), start=True, stop=True)
                last.then_inc(pv_ps, 1)

            def cross_turn(c):
                pe.wait_ge(x1n_sb, TPC * (c + 1))
                pe.wait_ge(vx_sb, c + 1)
                turn(g_bank[1], by_block(x1n), x1nT_ps)

            def cross_gate(c):
                pe.wait_ge(x1nT_sb, c + 1)
                pe.wait_ge(x1_sb, c + 1)
                features(g_bank[0], wg_sb, 0, x1nT, w_ps)

            def cross_queries(c):
                for h in range(KT):
                    last = pe.matmul(g_bank[1][:, h * TOK:(h + 1) * TOK], gram_sb[:, h, :], x1nT[:, h, :],
                                     start=True, stop=True)
                last.then_inc(qp_ps, 1)

            def cross_scores(c):
                pe.wait_ge(qp_sb, c + 1)
                for t in range(TPC):
                    for h in range(KT):
                        last = pe.matmul(c_bank[:, h * P:(h + 1) * P], ctxT[:, h, t * P:(t + 1) * P],
                                         qpT[:, h, t * P:(t + 1) * P], start=False, stop=True,
                                         skip_group_check=True)
                last.then_inc(sc_ps, 1)

            def attention(i, first, last):
                started = not first
                scores(i, 0, started)
                scores(i, 1, started)
                if not first:
                    cross_turn(i - 1)
                scores(i, 2, started)
                turn_probs(i, 0, started)
                scores(i, 3, started)
                turn_probs(i, 1, started)
                values(i, 0, started)
                if not first:
                    cross_gate(i - 1)
                turn_probs(i, 2, started)
                values(i, 1, started)
                if not first:
                    cross_queries(i - 1)
                turn_probs(i, 3, started)
                values(i, 2, started)
                values(i, 3, started)
                if not first:
                    cross_scores(i - 1)
                if not last:
                    pe.wait_ge(hn_sb, TPC * (i + 2))
                    if first:
                        pe.wait_ge(turned_out, 5)
                    else:
                        pe.wait_ge(w_sb, i)
                    turn(g_bank[0], by_block(hn), hT_ps)
                if first:
                    pe.wait_ge(turned_out, 4)
                else:
                    pe.wait_ge(qp_sb, i)
                pe.wait_ge(ld_ctx, 16 * (i + 1))
                turn(g_bank[1], by_block(ctx_sb), ctxT_ps)
                if not last:
                    pe.wait_ge(hT_sb, i + 2)
                    features(g_bank[0], wqkv_sb, D, hT, k_ps)
                    pe.wait_ge(ctxT_sb, i + 1)
                    features(g_bank[1], wqkv_sb, 0, hT, q_ps)
                    pe.wait_ge(k_sb, i + 2)
                    tokens(g_bank[0], hT, wqkv_sb, 2 * D, v_ps)
                    pe.wait_ge(q_sb, i + 2)
                else:
                    pe.wait_ge(ctxT_sb, i + 1)
                pe.wait_ge(att_sb, TPC * (i + 1))
                turn(g_bank[1], by_block(att), attT_ps)
                pe.wait_ge(attT_sb, i + 1)
                if not last:
                    pe.wait_ge(v_sb, i + 2)
                else:
                    pe.wait_ge(w_sb, i)
                tokens(g_bank[0], attT, wout_sb, 0, y_ps)
                for h in range(KT):
                    for t in range(TPC):
                        mm = pe.matmul(g_bank[1][:, h * TOK + t * P:h * TOK + (t + 1) * P],
                                       ctxT[:, h, t * P:(t + 1) * P], wh_sb[:, h, :], start=True, stop=True)
                mm.then_inc(vx_ps, 1)

            pe.wait_ge(ld_const, 16 * LOADS_CONST)
            pe.wait_ge(hn_sb, TPC)
            turn(g_bank[0], by_block(hn), hT_ps)
            pe.wait_ge(ld_wqkv, 16)
            pe.wait_ge(hT_sb, 1)
            features(g_bank[1], wqkv_sb, D, hT, k_ps)
            features(g_bank[0], wqkv_sb, 0, hT, q_ps)
            pe.wait_ge(k_sb, 1)
            tokens(g_bank[1], hT, wqkv_sb, 2 * D, v_ps)
            pe.wait_ge(ld_w, 16 * LOADS_W)
            pe.wait_ge(q_sb, 1)
            for h in range(KT):
                mm = pe.transpose(g_bank[0][:, h * P:(h + 1) * P], wh_sb[:, h, :], ident[:, :])
            mm.then_inc(turned, 1)
            pe.wait_ge(v_sb, 1)
            turn(g_bank[1], by_block(wup_sb), turned)
            pe.wait_ge(turned_out, 1)
            turn(g_bank[0], by_block(wdn_sb), turned)
            pe.wait_ge(turned_out, 2)
            for k in range(KT):
                mm = pe.transpose(g_bank[1][:, k * E:(k + 1) * E], wgate_sb[:, k * P:(k + 1) * P], ident[0:E, 0:E])
            mm.then_inc(turned, 1)
            pe.wait_ge(turned_out, 3)
            for h in range(KT):
                mm = pe.matmul(g_bank[0][:, h * P:(h + 1) * P], whT_sb[:, h, :], whT_sb[:, h, :], start=True, stop=True)
            mm.then_inc(turned, 1)
            pe.wait_ge(pool_const, 4)
            pe.matmul(c_bank[:, 0:KT * P], zeros[:, 0:P], zeros[:, 0:KT * P], start=True, stop=True,
                      skip_group_check=True)

            attention(0, True, False)
            with pe.Fori(1, NC - 1) as i:
                attention(i, False, False)
            attention(NC - 1, False, True)
            cross_turn(NC - 1)
            cross_gate(NC - 1)
            cross_queries(NC - 1)
            cross_scores(NC - 1)

            def cross_out(c):
                if type(c) is not int or c > 0:
                    pe.wait_ge(on_sb, TPC * c)
                for h in range(KT):
                    mm = pe.matmul(o_bank[:, :].rearrange("p (t h e) -> p t h e", t=TPC, h=KT)[:, :, h, :],
                                   aT[:, h, :], v_all[:, h, c, :], start=True, stop=True)
                mm.then_inc(o_ps, 1)

            def second(c, head, tail, more):
                if head:
                    pe.wait_ge(x2n_sb, TPC * c)
                    turn(t_bank[1], by_block(x2n), x2nT_ps)
                if tail:
                    pe.wait_ge(on_sb, TPC * (c + 1))
                    turn(t_bank[0], by_block(on), yT_ps)
                if more:
                    cross_out(c + 1)
                if head:
                    pe.wait_ge(x2nT_sb, c)
                    features(s_bank[0], wupT_sb, 0, x2nT, up_ps)
                if tail:
                    pe.wait_ge(zT_sb, c + 1)
                    tokens(g_bank[1], zT, wo_sb, 0, z_ps)
                if head:
                    if type(c) is not int or c > 1:
                        pe.wait_ge(out_sb, TPC * (c - 1))
                    for t, bank in enumerate((s_bank[1], g_bank[0])):
                        for k in range(KT):
                            mm = pe.matmul(bank[:, 0:D + E], x2nT[:, k, t * P:(t + 1) * P], wex_sb[:, k, :],
                                           start=(k == 0), stop=(k == KT - 1))
                    mm.then_inc(ex_ps, 1)
                    pe.wait_ge(uT_sb, c)
                    tokens(c_bank, uT, wdnT_sb, 0, dn_ps)

            pe.wait_ge(aT_sb, 1)
            cross_out(0)
            second(0, False, True, True)
            second(1, True, True, True)
            with pe.Fori(2, NC - 1) as c:
                second(c, True, True, True)
            second(NC - 1, True, True, False)
            second(NC, True, False, False)


def kernel(**inputs):
    import ml_dtypes
    import numpy as np
    import concourse.bacc as _bacc
    from concourse import mybir as _mybir
    from concourse.bass_utils import run_bass_kernel_spmd as _run

    a = {n: np.ascontiguousarray(v) for n, v in inputs.items()}
    b_qkv = a["L0_attn_b_qkv"]
    d = b_qkv.size // 3
    s = a["x"].shape[1]

    window = 64
    mask_sel = np.zeros((P, P), ml_dtypes.bfloat16)
    mask_sel[np.arange(P) % window, np.arange(P)] = 1
    mask = np.zeros((P, window), ml_dtypes.bfloat16)
    mask[:window][np.triu_indices(window, 1)] = -1e30
    heads = a["L0_xattn_Wh"].shape[0]
    hd = a["L0_xattn_Wh"].shape[1]
    gam = (1.0 - 2.0 ** (-5.0 - np.arange(heads))).astype(np.float32)
    idx = np.arange(s, dtype=np.float32)
    expo = idx[None, :] - idx[:, None]
    dm = np.where(expo[None] <= 0, gam[:, None, None] ** expo[None], np.float32(0)).astype(np.float32)
    dm = dm / np.sqrt(dm.sum(axis=-1))[:, None, :]
    decay = np.ascontiguousarray((dm / np.sqrt(np.float32(hd))).transpose(2, 0, 1), np.float32)

    arrays = {
        "x": a["x"], "ctx": a["ctx_2048"], "w_qkv": a["L0_attn_W_qkv"],
        "b_qk": b_qkv[:2 * d].reshape(2 * d // P, P).T,
        "b_v": np.broadcast_to(b_qkv[2 * d:], (P, d)),
        "w_out": a["L0_attn_W_out"], "b_out": np.broadcast_to(a["L0_attn_b_out"], (P, d)),
        "wh": a["L0_xattn_Wh"], "wg": a["L0_xattn_wg_w"], "wo": a["L0_xattn_wo_w"],
        "gamma": a["L0_xattn_gn_gamma"].reshape(d // P, P).T, "beta": a["L0_xattn_gn_beta"].reshape(d // P, P).T,
        "w_up": a["L0_ffn_W_up"], "w_down": a["L0_ffn_W_down"], "w_gate": a["L0_ffn_W_gate"],
        "w_expert": a["L0_ffn_W_expert"],
        "ident": np.eye(P, dtype=np.float32), "mask_sel": mask_sel, "mask": mask, "decay": decay,
    }
    arrays = {f"in_{n}_dram": np.ascontiguousarray(v) for n, v in arrays.items()}
    nc = _bacc.Bacc("TRN2", target_bir_lowering=False, num_devices=1)
    args = [nc.dram_tensor(n, v.shape, _mybir.dt.from_np(v.dtype), kind="ExternalInput").ap()
            for n, v in arrays.items()]
    args.append(nc.dram_tensor("out_0_dram", a["x"].shape, _mybir.dt.from_np(a["x"].dtype),
                               kind="ExternalOutput").ap())
    bass_decoder_layer_kernel(nc, *args)
    r = _run(nc, [arrays], core_ids=[0])
    return r.results[0]["out_0_dram"]
```

```python
from contextlib import ExitStack

import concourse.bass as bass
from concourse import mybir

ALU = mybir.AluOpType
ACT = mybir.ActivationFunctionType
F32 = mybir.dt.float32
F32R = mybir.dt.float32r
BF16 = mybir.dt.bfloat16
AX_X = mybir.AxisListType.X

P = 128
LN_EPS = 1e-5
GN_EPS = 1e-3
WINDOW = 64
HEADS = 16
DH = 16
ATT_SCALE = float(DH) ** -0.5


def bass_decoder_layer_kernel(nc, x, ctx_in, first_in, w_qkv, const_in, weights_in, mask_in, out):
    B, S, D = x.shape
    KT = D // P
    TPC = 2
    NC = B // TPC
    TOK = TPC * P
    NW = S // WINDOW
    HPH = HEADS // KT
    PAIRS = HEADS // 2
    VW = DH + 1
    W2 = KT * D
    E = weights_in.shape[1] // KT - 6 * D
    W_EX = KT * (D + E)
    STEPS = NC - 2
    PART = (3 * W2 + W_EX) // STEPS
    assert S == P and D == 2 * P and NW == 2 and PART * STEPS == 3 * W2 + W_EX

    with ExitStack() as ctx:
        def sb(name, shape, dt=F32):
            return ctx.enter_context(nc.sbuf_tensor(name, shape, dt))

        def pb(name):
            return ctx.enter_context(nc.psum_tensor(name, [P, 512], F32))

        def sem(name):
            return ctx.enter_context(nc.semaphore(name))

        def pair(name, shape):
            return sb(name + "_hi", shape, F32R), sb(name + "_lo", shape, F32R)

        x_all = sb("x_all", [P, NC, TPC * D])
        v_all = sb("v_all", [P, KT, NC, TOK])
        wT_all = sb("wT_all", [P, KT, NC, TOK])
        first_sb = sb("first_sb", [P, P + 2 * KT + HPH])
        wqkv_raw = sb("wqkv_raw", [P, KT, 3 * D])
        wqkv = pair("wqkv", [P, KT, 3 * D])
        const_sb = sb("const_sb", list(const_in.shape))
        w_raw = sb("w_raw", [P, 2 * W2 + STEPS * PART])
        wag = pair("wag", [P, 2, KT, D])
        later = pair("later", [P, STEPS, PART])
        gram_sb = sb("gram_sb", [P, KT, P])
        gram = pair("gram", [P, KT, P])
        mask_sb = sb("mask_sb", [P, P + WINDOW], BF16)
        zeros = sb("zeros", [P, 2 * P], BF16)
        minus_half, minus_one, ln_eps, gn_eps = (
            sb(n, [P, TPC]) for n in ("minus_half", "minus_one", "ln_eps", "gn_eps"))
        hn = sb("hn", [P, TPC, D])
        hT = pair("hT", [P, KT, TOK])
        kT = sb("kT", [P, KT, TOK])
        qT = sb("qT", [P, KT, TOK])
        k_heads = sb("k_heads", [P, KT, HPH, TOK])
        v_pairs = sb("v_pairs", [P, TPC, NW, PAIRS, 2, VW])
        probs = [sb(f"probs{n}", [P, HPH, WINDOW]) for n in range(2)]
        probsT = [sb(f"probsT{n}", [P, 512]) for n in range(2)]
        rowmax = sb("rowmax", [P, 2, HPH])
        rsum = sb("rsum", [P, TPC, HEADS])
        att = sb("att", [P, TPC, D])
        attT = pair("attT", [P, KT, TOK])
        x1n = sb("x1n", [P, TPC, D])
        x1nT = pair("x1nT", [P, KT, TOK])
        qpT = sb("qpT", [P, KT, TOK])
        ctxT = sb("ctxT", [P, KT, TOK])
        ctxT_last = sb("ctxT_last", [P, KT, TOK])
        bn1, bn2, bn4 = (sb(f"bn{n}", [P, TPC, 6]) for n in (1, 2, 4))
        mv1, mv2, mv4 = (sb(f"mv{n}", [P, TPC, 2]) for n in (1, 2, 4))
        rs1, rs2, rs4 = (sb(f"rs{n}", [P, TPC]) for n in (1, 2, 4))
        ve1, ve2, ve4 = (sb(f"ve{n}", [P, TPC]) for n in (1, 2, 4))
        norm_of_o = [tuple(sb(f"{n}{m}", [P, TPC, w] if w else [P, TPC]) for n, w in
                           (("bno", 6), ("mvo", 2), ("veo", 0), ("rso", 0), ("neg_mean", 0), ("shift", 0)))
                     for m in range(2)]
        dec = sb("dec", [P, KT * P])
        dabs = sb("dabs", [P, KT * P])
        aT = sb("aT", [P, KT, P])
        on = sb("on", [P, TPC, D])
        yT = sb("yT", [P, KT, TOK])
        z_full = sb("z_full", [P, KT, TOK])
        zT = pair("zT", [P, KT, TOK])
        x2n = sb("x2n", [P, TPC, D])
        x2nT = pair("x2nT", [P, KT, TOK])
        uT = pair("uT", [P, KT, TOK])
        moe = sb("moe", [P, TPC, D])
        top = sb("top", [P, TPC, 8])
        ldiff, esec, eden, einv, rw = (sb(n, [P, TPC]) for n in ("ldiff", "esec", "eden", "einv", "rw"))

        ident = first_sb[:, 0:P]
        bqk_sb = first_sb[:, P:P + 2 * KT]
        head_rows = first_sb[:, P + 2 * KT:P + 2 * KT + HPH]
        bv_sb = const_sb[:, 0:D]
        bout_sb = const_sb[:, D:2 * D]
        decay = const_sb[:, 2 * D:2 * D + KT * P]
        wh_sb = const_sb[:, 3 * D:4 * D].rearrange("p (h e) -> p h e", h=KT)
        whT_sb = const_sb[:, 4 * D:5 * D].rearrange("p (h e) -> p h e", h=KT)
        gb_sb = const_sb[:, 5 * D:5 * D + 2 * KT]
        mask_sel = mask_sb[:, 0:P]
        mask = mask_sb[:, P:P + WINDOW]

        def part_of(packed, first, width):
            return tuple(p.rearrange("p a b -> p (a b)")[:, first:first + KT * width]
                         .rearrange("p (k n) -> p k n", k=KT) for p in (packed[0][:, :, :], packed[1][:, :, :]))

        wout = tuple(p[:, 0] for p in wag)
        wg = tuple(p[:, 1] for p in wag)
        wo = part_of(later, 0, D)
        wup = part_of(later, W2, D)
        wdn = part_of(later, 2 * W2, D)
        wex = part_of(later, 3 * W2, D + E)

        s_bank = [pb("s_bank0"), pb("s_bank1")]
        t_bank = [pb("t_bank0"), pb("t_bank1")]
        o_bank = pb("o_bank")
        g_bank = [pb("g_bank0"), pb("g_bank1")]
        c_bank = pb("c_bank")

        ld_x0, ld_x, ld_ctx, ld_ctx_last, ld_first, ld_wqkv, ld_mask, ld_const, ld_w = map(
            sem, "ld_x0 ld_x ld_ctx ld_ctx_last ld_first ld_wqkv ld_mask ld_const ld_w".split())
        zeros_set, small_set, pool_const, first_keys = map(sem, "zeros_set small_set pool_const first_keys".split())
        wqkv_hi, wqkv_lo, wag_hi, wag_lo, later_hi, later_lo = map(
            sem, "wqkv_hi wqkv_lo wag_hi wag_lo later_hi later_lo".split())
        gram_ps, gram_sb_done, gram_hi, gram_lo = map(sem, "gram_ps gram_sb_done gram_hi gram_lo".split())
        hT_ps, k_ps, q_ps, v_ps, attT_ps, y_ps = map(sem, "hT_ps k_ps q_ps v_ps attT_ps y_ps".split())
        x1nT_ps, w_ps, qp_ps, vx_ps, sc_ps = map(sem, "x1nT_ps w_ps qp_ps vx_ps sc_ps".split())
        s_ps, pT_ps, pv_ps = map(sem, "s_ps pT_ps pv_ps".split())
        k_sb, q_sb, v_sb, x1_sb, w_sb, qp_sb, vx_sb = map(sem, "k_sb q_sb v_sb x1_sb w_sb qp_sb vx_sb".split())
        hT_hi, hT_lo, attT_hi, attT_lo, x1nT_hi, x1nT_lo = map(
            sem, "hT_hi hT_lo attT_hi attT_lo x1nT_hi x1nT_lo".split())
        max_sb, sub_sb, exp_sb, pT_sb, rsum_sb, att_sb = map(sem, "max_sb sub_sb exp_sb pT_sb rsum_sb att_sb".split())
        kh_dma = sem("kh_dma")
        ag1, pe1, ps1, hn_sb, xb_sb = map(sem, "ag1 pe1 ps1 hn_sb xb_sb".split())
        ag2, pe2, ps2, x1n_sb = map(sem, "ag2 pe2 ps2 x1n_sb".split())
        ag3, nm3, pe3, ps3, sh3, on_sb = map(sem, "ag3 nm3 pe3 ps3 sh3 on_sb".split())
        ag4, pe4, ps4, x2n_sb = map(sem, "ag4 pe4 ps4 x2n_sb".split())
        dec_sb, abs_sb, aT_sb = map(sem, "dec_sb abs_sb aT_sb".split())
        o_ps, yT_ps, z_ps, x2nT_ps, up_ps, ex_ps, dn_ps = map(sem, "o_ps yT_ps z_ps x2nT_ps up_ps ex_ps dn_ps".split())
        yT_sb, z_sb, zT_hi, zT_lo, x2_sb = map(sem, "yT_sb z_sb zT_hi zT_lo x2_sb".split())
        x2nT_hi, x2nT_lo, uT_hi, uT_lo = map(sem, "x2nT_hi x2nT_lo uT_hi uT_lo".split())
        top_sb, ld_sb, es_sb, ed_sb, ei_sb, rw_sb, moe_sb, acc_sb, out_sb = map(
            sem, "top_sb ld_sb es_sb ed_sb ei_sb rw_sb moe_sb acc_sb out_sb".split())
        st_out = sem("st_out")

        out_dram = out.rearrange("(c t) s d -> s c t d", t=TPC)
        x_dram = x.rearrange("(c t) s d -> s c t d", t=TPC)

        def tiles(ap):
            return ap.rearrange("p (t d) -> p t d", t=TPC)

        def halves(bank, n=512):
            return bank[:, 0:n].rearrange("p (k n) -> p k n", k=KT)

        UNITS = TPC * KT
        NK = HPH
        WAKE = 26
        DVE_BLOCKS, ACT_BLOCKS, POOL_BLOCKS = range(0, 4), range(4, 7), range(7, 8)
        EX_BANKS = (s_bank[1], g_bank[0])

        block = ctx.enter_context(nc.Block())

        @block.sync
        def _(sp):
            sp.dma_start(tiles(x_all[:, 0, :]), x_dram[:, 0]).then_inc(ld_x0, 16)
            sp.dma_start(wqkv_raw[:, :, :], w_qkv.rearrange("(k p) n -> p k n", p=P)).then_inc(ld_wqkv, 16)
            sp.dma_start(mask_sb[:, :], mask_in).then_inc(ld_mask, 16)
            sp.dma_start(x_all[:, 1:NC, :].rearrange("p c (t d) -> p c t d", t=TPC), x_dram[:, 1:NC]).then_inc(ld_x, 16)
            sp.dma_start(w_raw[:, :], weights_in[:, 0:w_raw.shape[1]]).then_inc(ld_w, 16)
            sp.dma_start(ctxT[:, :, :], ctx_in[0]).then_inc(ld_ctx, 16)
            sp.dma_start(ctxT_last[:, :, :], ctx_in[NC - 1]).then_inc(ld_ctx_last, 16)

            def spread_keys(c):
                sp.wait_ge(k_sb, c + 1)
                sp.wait_ge(s_ps, UNITS * c)
                for h in range(HPH):
                    rows = slice(DH * h, DH * h + DH)
                    sp.dma_start(k_heads[rows, :, h, :], kT[rows, :, :]).then_inc(kh_dma, 16)

            sp.wait_ge(first_keys, HPH)
            spread_keys(1)
            with sp.Fori(1, NC - 1) as c:
                spread_keys(c + 1)
                sp.wait_ge(sc_ps, c)
                sp.wait_ge(vx_ps, c)
                sp.dma_start(ctxT[:, :, :], ctx_in[c]).then_inc(ld_ctx, 16)
            with sp.Fori(0, NC) as c:
                sp.wait_ge(out_sb, c + 1)
                sp.dma_start(out_dram[:, c], tiles(x_all[:, c, :])).then_inc(st_out, 16)
            sp.wait_ge(st_out, 16 * NC)

        @block.gpsimd
        def _(pool):
            pool.memset(zeros[:, :], 0.0).then_inc(zeros_set, 1)
            pool.memset(minus_half[:, :], -0.5)
            pool.memset(minus_one[:, :], -1.0)
            pool.memset(ln_eps[:, :], LN_EPS)
            pool.memset(gn_eps[:, :], GN_EPS).then_inc(small_set, 1)
            pool.wait_ge(small_set, 1)

            def rsqrt(c, mv, ve, rs, ag, pe, ps, eps):
                pool.wait_ge(ag, TPC * (c + 1))
                pool.tensor_tensor(ve[:, :], mv[:, :, 1], eps[:, :], ALU.add).then_inc(pe, 1)
                pool.wait_ge(pe, c + 1)
                pool.tensor_tensor(rs[:, :], ve[:, :], minus_half[:, :], ALU.pow).then_inc(ps, 1)

            def norm1(c):
                rsqrt(c, mv1, ve1, rs1, ag1, pe1, ps1, ln_eps)

            def add_bias(c):
                pool.wait_ge(hn_sb, TPC * (c + 1))
                for t in range(TPC):
                    xt = x_all[:, c, t * D:(t + 1) * D]
                    pool.tensor_tensor(xt, xt, bout_sb, ALU.add).then_inc(xb_sb, 1)

            def split_later(s):
                raw = w_raw[:, 2 * W2:].rearrange("p (a b) -> p a b", b=PART)[:, s, :]
                pool.tensor_copy(later[0][:, s, :], raw).then_inc(later_hi, 1)
                pool.wait_ge(later_hi, s + 1)
                pool.tensor_tensor(later[1][:, s, :], raw, later[0][:, s, :].bitcast(F32),
                                   ALU.subtract).then_inc(later_lo, 1)

            norm1(0)
            pool.memset(v_pairs[:, :, :, :, :, :], 0.0).then_inc(pool_const, 1)
            pool.wait_ge(pool_const, 1)
            for h in range(2):
                rows = slice(WINDOW * h, WINDOW * h + WINDOW)
                pool.memset(v_pairs[rows, :, :, :, h, DH:VW], 1.0).then_inc(pool_const, 1)
                pool.wait_ge(pool_const, 2 + h)
            norm1(1)
            pool.wait_ge(ld_first, 16)
            pool.wait_ge(k_sb, 1)
            for h in POOL_BLOCKS:
                pool.tensor_tensor(k_heads[:, :, h, :], kT[:, :, :],
                                   head_rows[:, h:h + 1].unsqueeze(2).broadcast_to([P, KT, TOK]),
                                   ALU.mult).then_inc(first_keys, 1)
            pool.wait_ge(ld_w, 16)
            for m in range(2):
                raw = w_raw[:, m * W2:(m + 1) * W2].rearrange("p (k n) -> p k n", k=KT)
                pool.tensor_copy(wag[0][:, m], raw).then_inc(wag_hi, 1)
                pool.wait_ge(wag_hi, m + 1)
                pool.tensor_tensor(wag[1][:, m], raw, wag[0][:, m].bitcast(F32), ALU.subtract).then_inc(wag_lo, 1)
            pool.wait_ge(gram_sb_done, 1)
            pool.tensor_copy(gram[0][:, :, :], gram_sb[:, :, :]).then_inc(gram_hi, 1)
            pool.wait_ge(gram_hi, 1)
            pool.tensor_tensor(gram[1][:, :, :], gram_sb[:, :, :], gram[0][:, :, :].bitcast(F32),
                               ALU.subtract).then_inc(gram_lo, 1)
            pool.wait_ge(ld_const, 16)
            add_bias(0)
            add_bias(1)

            def attention(i, more):
                if more:
                    norm1(i + 2)
                    split_later(i)
                    add_bias(i + 2)
                rsqrt(i, mv2, ve2, rs2, ag2, pe2, ps2, ln_eps)

            with pool.Fori(0, NC - 2) as i:
                attention(i, True)
            attention(NC - 2, False)
            attention(NC - 1, False)

            def norm3(c, which=0):
                _, mv, ve, rs, neg_mean, shift = norm_of_o[which]
                pool.wait_ge(ag3, TPC * (c + 1))
                if type(c) is not int:
                    pool.wait_ge(sh3, c)
                pool.tensor_tensor(neg_mean[:, :], mv[:, :, 0], minus_one[:, :], ALU.mult).then_inc(nm3, 1)
                rsqrt(c, mv, ve, rs, ag3, pe3, ps3, gn_eps)
                pool.wait_ge(nm3, c + 1)
                pool.wait_ge(ps3, c + 1)
                pool.tensor_tensor(shift[:, :], neg_mean[:, :], rs[:, :], ALU.mult).then_inc(sh3, 1)

            def gate(c):
                for k in range(KT):
                    pool.wait_ge(yT_sb, KT * c + k + 1)
                    pool.tensor_tensor(z_full[:, k, :], yT[:, k, :], wT_all[:, k, c, :], ALU.mult).then_inc(z_sb, 1)

            def gate_lo(c):
                pool.wait_ge(zT_hi, c + 1)
                pool.tensor_tensor(zT[1][:, :, :], z_full[:, :, :], zT[0][:, :, :].bitcast(F32),
                                   ALU.subtract).then_inc(zT_lo, 1)

            def norm4(c):
                rsqrt(c, mv4, ve4, rs4, ag4, pe4, ps4, ln_eps)

            def add_moe(c):
                pool.wait_ge(moe_sb, TPC * (c + 1))
                pool.tensor_tensor(x_all[:, c, :], x_all[:, c, :], moe[:, :, :].rearrange("p t d -> p (t d)"),
                                   ALU.add).then_inc(acc_sb, 1)

            norm3(0)
            norm3(1, 1)
            gate(0)
            gate_lo(0)
            norm4(0)
            gate(1)
            gate_lo(1)
            norm3(2)
            norm4(1)
            gate(2)
            gate_lo(2)
            with pool.Fori(2, NC - 1) as j:
                norm3(j + 1)
                add_moe(j - 2)
                norm4(j)
                gate(j + 1)
                gate_lo(j + 1)
            add_moe(NC - 3)
            norm4(NC - 1)
            add_moe(NC - 2)
            add_moe(NC - 1)

        @block.scalar
        def _(act):
            act.dma_start(first_sb[:, :], first_in).then_inc(ld_first, 16)
            act.dma_start(const_sb[:, :], const_in).then_inc(ld_const, 16)

            def copy_out(c, filled, bank, dst, done):
                act.wait_ge(filled, c + 1)
                act.activation(dst, halves(bank), ACT.Copy).then_inc(done, 1)

            def hT_out(c):
                copy_out(c, hT_ps, g_bank[0], hT[0][:, :, :], hT_hi)

            def k_out(c, bank):
                act.wait_ge(k_ps, c + 1)
                for k in range(KT):
                    last = act.activation(kT[:, k, :], halves(bank)[:, k, :], ACT.Identity,
                                          bias=bqk_sb[:, KT + k:KT + k + 1])
                last.then_inc(k_sb, 1)

            def q_out(c, bank):
                act.wait_ge(q_ps, c + 1)
                for k in range(KT):
                    last = act.activation(qT[:, k, :], halves(bank)[:, k, :], ACT.Identity,
                                          bias=bqk_sb[:, k:k + 1])
                last.then_inc(q_sb, 1)

            def exps(i, u):
                act.wait_ge(sub_sb, UNITS * i + u + 1)
                p = probs[u % 2]
                act.activation(p[:, :, :], p[:, :, :], ACT.Exp, scale=ATT_SCALE).then_inc(exp_sb, 1)

            def probsT_out(i, u):
                act.wait_ge(pT_ps, UNITS * i + u + 1)
                act.activation(probsT[u % 2][:, :], t_bank[u % 2][:, :], ACT.Copy).then_inc(pT_sb, 1)

            def gate_out(c, bank):
                act.wait_ge(w_ps, c + 1)
                act.activation(wT_all[:, :, c, :], halves(bank), ACT.Relu).then_inc(w_sb, 1)

            def attention(i, first, last):
                exps(i, 0)
                if not last:
                    hT_out(i + 1)
                exps(i, 1)
                probsT_out(i, 0)
                exps(i, 2)
                if not last:
                    k_out(i + 1, g_bank[1])
                probsT_out(i, 1)
                exps(i, 3)
                if not last:
                    act.wait_ge(s_ps, UNITS * (i + 1))
                    q_out(i + 1, g_bank[0])
                probsT_out(i, 2)
                if not first:
                    copy_out(i - 1, x1nT_ps, g_bank[1], x1nT[0][:, :, :], x1nT_hi)
                probsT_out(i, 3)
                if not first:
                    if not last:
                        gate_out(i - 1, g_bank[1])
                    copy_out(i - 1, qp_ps, t_bank[0], qpT[:, :, :], qp_sb)
                copy_out(i, attT_ps, g_bank[0], attT[0][:, :, :], attT_hi)
                if not first:
                    if last:
                        gate_out(i - 1, g_bank[1])
                    copy_out(i - 1, vx_ps, g_bank[0], v_all[:, :, i - 1, :], vx_sb)

            act.wait_ge(ld_first, 16)
            act.wait_ge(ld_wqkv, 16)
            for m in (1, 0, 2):
                act.activation(wqkv[0][:, :, m * D:(m + 1) * D], wqkv_raw[:, :, m * D:(m + 1) * D],
                               ACT.Copy).then_inc(wqkv_hi, 1)
                if m == 1:
                    hT_out(0)
            k_out(0, g_bank[1])
            act.wait_ge(k_sb, 1)
            for h in ACT_BLOCKS:
                act.activation(k_heads[:, :, h, :], kT[:, :, :], ACT.Copy,
                               scale=head_rows[:, h:h + 1]).then_inc(first_keys, 1)
            q_out(0, g_bank[0])
            act.wait_ge(gram_ps, 1)
            act.activation(gram_sb[:, :, :], halves(g_bank[0], KT * P), ACT.Copy).then_inc(gram_sb_done, 1)

            attention(0, True, False)
            with act.Fori(1, NC - 1) as i:
                attention(i, False, False)
            attention(NC - 1, False, True)
            copy_out(NC - 1, vx_ps, t_bank[1], v_all[:, :, NC - 1, :], vx_sb)
            copy_out(NC - 1, x1nT_ps, g_bank[1], x1nT[0][:, :, :], x1nT_hi)
            copy_out(NC - 1, qp_ps, s_bank[1], qpT[:, :, :], qp_sb)
            gate_out(NC - 1, g_bank[0])

            def y_out(c):
                act.wait_ge(yT_ps, c + 1)
                if type(c) is not int or c > 0:
                    act.wait_ge(z_sb, KT * c)
                for k in range(KT):
                    act.activation(yT[:, k, :], halves(t_bank[0])[:, k, :], ACT.Identity,
                                   scale=gb_sb[:, k:k + 1], bias=gb_sb[:, KT + k:KT + k + 1]).then_inc(yT_sb, 1)

            def on_out(c, bank, which=0):
                rs, shift = norm_of_o[which][3], norm_of_o[which][5]
                act.wait_ge(sh3, c + 1)
                if type(c) is not int or c > 0:
                    act.wait_ge(yT_ps, c)
                for t in range(TPC):
                    act.activation(on[:, t, :], bank[:, t * D:(t + 1) * D], ACT.Identity,
                                   scale=rs[:, t:t + 1], bias=shift[:, t:t + 1]).then_inc(on_sb, 1)

            def z_hi(c):
                act.wait_ge(z_sb, KT * (c + 1))
                act.activation(zT[0][:, :, :], z_full[:, :, :], ACT.Copy).then_inc(zT_hi, 1)

            def x2nT_out(c):
                copy_out(c, x2nT_ps, t_bank[1], x2nT[0][:, :, :], x2nT_hi)

            def u_out(c):
                act.wait_ge(up_ps, c + 1)
                act.activation(uT[0][:, :, :], halves(s_bank[0]), ACT.Relu).then_inc(uT_hi, 1)

            def exp_out(c):
                act.wait_ge(ld_sb, c + 1)
                act.activation(esec[:, :], ldiff[:, :], ACT.Exp).then_inc(es_sb, 1)

            def moe_out(c):
                act.wait_ge(rw_sb, c + 1)
                for t, bank in enumerate(EX_BANKS):
                    act.activation(moe[:, t, :], bank[:, 0:D], ACT.Copy, scale=rw[:, t:t + 1]).then_inc(moe_sb, 1)

            on_out(0, o_bank)
            on_out(1, t_bank[1], 1)
            y_out(0)
            y_out(1)
            z_hi(0)
            z_hi(1)
            with act.Fori(1, NC - 1) as j:
                x2nT_out(j - 1)
                on_out(j + 1, o_bank)
                u_out(j - 1)
                y_out(j + 1)
                exp_out(j - 1)
                z_hi(j + 1)
                moe_out(j - 1)
            x2nT_out(NC - 2)
            u_out(NC - 2)
            exp_out(NC - 2)
            moe_out(NC - 2)
            x2nT_out(NC - 1)
            u_out(NC - 1)
            exp_out(NC - 1)
            moe_out(NC - 1)

        @block.vector
        def _(dve):
            def norm_stats(c, src, bn, mv, ag, source=None):
                dve.wait_ge(ld_x0, 16)
                if source is not None:
                    dve.wait_ge(source, c + 1)
                for t in range(TPC):
                    dve.bn_stats(bn[:, t, :], src(t))
                dve.drain()
                for t in range(TPC):
                    dve.bn_aggr(mv[:, t, :], bn[:, t, :]).then_inc(ag, 1)

            def normalize(c, src, dst, mv, rs, ps, done):
                dve.wait_ge(ps, c + 1)
                for t in range(TPC):
                    dve.tensor_scalar(dst[:, t, :], src(t), mv[:, t, 0:1], rs[:, t:t + 1],
                                      ALU.subtract, ALU.mult).then_inc(done, 1)

            def x_tile(c):
                return lambda t: x_all[:, c, t * D:(t + 1) * D]

            def lo_out(c, hi_done, bank, parts, done):
                dve.wait_ge(hi_done, c + 1)
                dve.tensor_tensor(parts[1][:, :, :], halves(bank), parts[0][:, :, :].bitcast(F32),
                                  ALU.subtract).then_inc(done, 1)

            def soften(i, u, started):
                bank = s_bank[u % 2][:, :].rearrange("p (h k) -> p h k", h=HPH)
                dve.wait_ge(s_ps, UNITS * i + u + 1)
                dve.tensor_reduce(rowmax[:, u % 2, :], bank, AX_X, ALU.max).then_inc(max_sb, 1)
                dve.wait_ge(max_sb, UNITS * i + u + 1)
                if started or u >= 2:
                    dve.wait_ge(pT_ps, UNITS * i + u - 1)
                dve.tensor_tensor(probs[u % 2][:, :, :], bank,
                                  rowmax[:, u % 2, :].unsqueeze(2).broadcast_to([P, HPH, WINDOW]),
                                  ALU.subtract).then_inc(sub_sb, 1)

            def v_out(c, bank):
                dve.wait_ge(v_ps, c + 1)
                if type(c) is not int or c > 0:
                    dve.wait_ge(pv_ps, UNITS * c)
                src = bank[:, :].rearrange("p (t j h d) -> p t j h d", t=TPC, h=2, d=DH)
                bias = bv_sb.rearrange("p (j h d) -> p j h d", h=2, d=DH)
                for w in range(NW):
                    for h in range(2):
                        wr = slice(WINDOW * w, WINDOW * w + WINDOW)
                        hr = slice(WINDOW * h, WINDOW * h + WINDOW)
                        last = dve.tensor_tensor(
                            v_pairs[hr, :, w, :, h, 0:DH], src[wr, :, :, h, :],
                            bias[wr, :, h, :].unsqueeze(1).broadcast_to([WINDOW, TPC, PAIRS, DH]), ALU.add)
                last.then_inc(v_sb, 1)

            def att_out(i, t):
                o = o_bank[:, 0:HEADS * VW].rearrange("p (h v) -> p h v", v=VW)
                dve.wait_ge(pv_ps, UNITS * i + KT * (t + 1))
                dve.reciprocal(rsum[:, t, :], o[:, :, DH]).then_inc(rsum_sb, 1)
                dve.wait_ge(rsum_sb, TPC * i + t + 1)
                dve.tensor_tensor(att[:, t, :].rearrange("p (h d) -> p h d", d=DH), o[:, :, 0:DH],
                                  rsum[:, t, :].unsqueeze(2).broadcast_to([P, HEADS, DH]),
                                  ALU.mult).then_inc(att_sb, 1)

            def norm1_stats(c):
                norm_stats(c, x_tile(c), bn1, mv1, ag1)

            def norm1(c):
                normalize(c, x_tile(c), hn, mv1, rs1, ps1, hn_sb)

            def norm2(c):
                normalize(c, x_tile(c), x1n, mv2, rs2, ps2, x1n_sb)

            def norm2_stats(c):
                norm_stats(c, x_tile(c), bn2, mv2, ag2, x1_sb)

            def attention(i, first, more, last):
                soften(i, 0, not first)
                soften(i, 1, not first)
                if not last:
                    lo_out(i + 1, hT_hi, g_bank[0], hT, hT_lo)
                if not first:
                    norm2_stats(i - 1)
                soften(i, 2, not first)
                soften(i, 3, not first)
                if not first:
                    norm2(i - 1)
                att_out(i, 0)
                if not first:
                    lo_out(i - 1, x1nT_hi, g_bank[1], x1nT, x1nT_lo)
                if more:
                    norm1_stats(i + 2)
                if not last:
                    v_out(i + 1, g_bank[0])
                att_out(i, 1)
                lo_out(i, attT_hi, g_bank[0], attT, attT_lo)
                if more:
                    norm1(i + 2)
                dve.wait_ge(y_ps, i + 1)
                dve.wait_ge(xb_sb, TPC * (i + 1))
                dve.tensor_tensor(x_all[:, i, :], (s_bank[0] if last else g_bank[1])[:, :], x_all[:, i, :],
                                  ALU.add).then_inc(x1_sb, 1)

            norm1_stats(0)
            norm1(0)
            dve.wait_ge(ld_wqkv, 16)
            for n, m in enumerate((1, 0, 2)):
                dve.wait_ge(wqkv_hi, n + 1)
                at = slice(m * D, (m + 1) * D)
                dve.tensor_tensor(wqkv[1][:, :, at], wqkv_raw[:, :, at], wqkv[0][:, :, at].bitcast(F32),
                                  ALU.subtract).then_inc(wqkv_lo, 1)
                if m == 1:
                    lo_out(0, hT_hi, g_bank[0], hT, hT_lo)
            dve.wait_ge(ld_x, 16)
            norm1_stats(1)
            norm1(1)
            dve.wait_ge(ld_first, 16)
            dve.wait_ge(k_sb, 1)
            for h in DVE_BLOCKS:
                dve.tensor_scalar(k_heads[:, :, h, :], kT[:, :, :], head_rows[:, h:h + 1], None,
                                  ALU.mult).then_inc(first_keys, 1)
            dve.wait_ge(ld_const, 16)
            dve.wait_ge(pool_const, 3)
            v_out(0, g_bank[1])
            attention(0, True, True, False)
            with dve.Fori(1, NC - 2) as i:
                attention(i, False, True, False)
            attention(NC - 2, False, False, False)
            attention(NC - 1, False, False, True)
            norm2_stats(NC - 1)
            norm2(NC - 1)
            lo_out(NC - 1, x1nT_hi, g_bank[1], x1nT, x1nT_lo)

            dve.wait_ge(sc_ps, NC)
            dve.tensor_tensor(dec[:, :], c_bank[:, 0:KT * P], decay, ALU.mult).then_inc(dec_sb, 1)
            dve.wait_ge(dec_sb, 1)
            dve.scalar_tensor_tensor(out=dabs[:, :], in0=dec[:, :], scalar=-1.0, in1=dec[:, :],
                                     op0=ALU.mult, op1=ALU.max).then_inc(abs_sb, 1)
            dve.wait_ge(abs_sb, 1)
            dve.tensor_scalar(aT[:, :, :].rearrange("p k n -> p (k n)"), dabs[:, :], 1.0, None,
                              ALU.max).then_inc(aT_sb, 1)

            def o_stats(c, bank, which=0):
                bn, mv = norm_of_o[which][0:2]
                norm_stats(c, lambda t: bank[:, t * D:(t + 1) * D], bn, mv, ag3, o_ps)

            def x2_out(c):
                dve.wait_ge(z_ps, c + 1)
                dve.tensor_tensor(x_all[:, c, :], g_bank[1][:, :], x_all[:, c, :], ALU.add).then_inc(x2_sb, 1)
                norm_stats(c, x_tile(c), bn4, mv4, ag4, x2_sb)

            def norm4(c):
                normalize(c, x_tile(c), x2n, mv4, rs4, ps4, x2n_sb)

            def u_lo(c):
                dve.wait_ge(uT_hi, c + 1)
                dve.scalar_tensor_tensor(out=uT[1][:, :, :], in0=halves(s_bank[0]), scalar=0.0,
                                         in1=uT[0][:, :, :].bitcast(F32), op0=ALU.max,
                                         op1=ALU.subtract).then_inc(uT_lo, 1)

            def route(c):
                dve.wait_ge(ld_x0, 16)
                dve.wait_ge(ex_ps, c + 1)
                for t, bank in enumerate(EX_BANKS):
                    dve.max(top[:, t, :], bank[:, D:D + E]).then_inc(top_sb, 1)
                dve.wait_ge(top_sb, TPC * (c + 1))
                dve.tensor_tensor(ldiff[:, :], top[:, :, 1], top[:, :, 0], ALU.subtract).then_inc(ld_sb, 1)

            def weigh(c):
                dve.wait_ge(es_sb, c + 1)
                dve.tensor_scalar(eden[:, :], esec[:, :], 1.0, None, ALU.add).then_inc(ed_sb, 1)
                dve.wait_ge(ed_sb, c + 1)
                dve.reciprocal(einv[:, :], eden[:, :]).then_inc(ei_sb, 1)
                dve.wait_ge(ei_sb, c + 1)
                for t in range(TPC):
                    last = dve.scalar_tensor_tensor(out=rw[:, t:t + 1], in0=esec[:, t:t + 1], scalar=einv[:, t:t + 1],
                                                    in1=einv[:, t:t + 1], op0=ALU.mult, op1=ALU.add)
                last.then_inc(rw_sb, 1)

            def finish(c):
                dve.wait_ge(dn_ps, c + 1)
                dve.wait_ge(acc_sb, c + 1)
                dve.tensor_tensor(x_all[:, c, :], c_bank[:, :], x_all[:, c, :], ALU.add).then_inc(out_sb, 1)

            def second(j, x2nT_of, stats_of, add_to, finishes):
                if stats_of is not None:
                    o_stats(stats_of, o_bank)
                if x2nT_of is not None:
                    lo_out(x2nT_of, x2nT_hi, t_bank[1], x2nT, x2nT_lo)
                if add_to is not None:
                    x2_out(add_to)
                if finishes is not None:
                    finish(finishes)
                if x2nT_of is not None:
                    u_lo(x2nT_of)
                if add_to is not None:
                    norm4(add_to)
                if x2nT_of is not None:
                    route(x2nT_of)
                    weigh(x2nT_of)

            o_stats(0, o_bank)
            o_stats(1, t_bank[1], 1)
            second(0, None, None, 0, None)
            second(1, 0, 2, 1, None)
            with dve.Fori(2, NC - 1) as j:
                second(j, j - 1, j + 1, j, j - 2)
            second(NC - 1, NC - 2, None, NC - 1, NC - 3)
            second(NC, NC - 1, None, None, NC - 2)
            finish(NC - 1)

        @block.tensor
        def _(pe):
            def turn(bank, src, done):
                for k in range(KT):
                    for t in range(TPC):
                        last = pe.transpose(bank[:, k * TOK + t * P:k * TOK + t * P + P],
                                            src[:, t, k * P:(k + 1) * P], ident)
                last.then_inc(done, 1)

            def features(bank, w, col, srcT, done, lo=None):
                for f in range(KT):
                    at = slice(col + f * P, col + (f + 1) * P)
                    dst = bank[:, f * TOK:(f + 1) * TOK]
                    for k in range(KT):
                        pe.matmul(dst, w[0][:, k, at], srcT[0][:, k, :], start=(k == 0), stop=False)
                        pe.matmul(dst, w[1][:, k, at], srcT[0][:, k, :], start=False, stop=False)
                    if lo is not None and f == 0:
                        pe.wait_ge(*lo)
                    for k in range(KT):
                        last = pe.matmul(dst, w[0][:, k, at], srcT[1][:, k, :], start=False, stop=(k == KT - 1))
                last.then_inc(done, 1)

            def rows_by(bank, srcT, w, t, width, col, lo=None):
                rows = slice(t * P, (t + 1) * P)
                for k in range(KT):
                    pe.matmul(bank, srcT[0][:, k, rows], w[0][:, k, col:col + width], start=(k == 0), stop=False)
                    pe.matmul(bank, srcT[0][:, k, rows], w[1][:, k, col:col + width], start=False, stop=False)
                if lo is not None:
                    pe.wait_ge(*lo)
                for k in range(KT):
                    last = pe.matmul(bank, srcT[1][:, k, rows], w[0][:, k, col:col + width],
                                     start=False, stop=(k == KT - 1))
                return last

            def tokens(bank, srcT, w, col, done, lo=None):
                for t in range(TPC):
                    last = rows_by(bank[:, t * D:(t + 1) * D], srcT, w, t, D, col, lo if t == 0 else None)
                last.then_inc(done, 1)

            def scores(i, u, started):
                t, k = divmod(u, KT)
                bank = s_bank[u % 2]
                if started or u >= 2:
                    pe.wait_ge(sub_sb, UNITS * i + u - 1)
                pe.matmul(bank[:, :], mask_sel, mask.unsqueeze(1).broadcast_to([P, HPH, WINDOW]),
                          start=True, stop=False, skip_group_check=True)
                if u == 0:
                    if started:
                        pe.wait_ge(kh_dma, 16 * NK * i)
                    else:
                        pe.wait_ge(first_keys, HPH)
                    pe.wait_ge(q_sb, i + 1)
                for w in range(NW):
                    at = t * P + w * WINDOW
                    last = pe.matmul(bank[WINDOW * w:WINDOW * (w + 1), :], qT[:, k, at:at + WINDOW],
                                     k_heads[:, k, :, at:at + WINDOW], start=False, stop=True,
                                     skip_group_check=True)
                last.then_inc(s_ps, 1)

            def turn_probs(i, u, started):
                pe.wait_ge(exp_sb, UNITS * i + u + 1)
                if started or u >= 2:
                    pe.wait_ge(pT_sb, UNITS * i + u - 1)
                for j in range(HPH // 2):
                    src = probs[u % 2][:, 2 * j:2 * j + 2, :].rearrange("p h k -> p (h k)")
                    last = pe.transpose(t_bank[u % 2][:, j * P:(j + 1) * P], src, ident)
                last.then_inc(pT_ps, 1)

            def values(i, u, started):
                t, k = divmod(u, KT)
                pe.wait_ge(pT_sb, UNITS * i + u + 1)
                if u == 0:
                    pe.wait_ge(v_sb, i + 1)
                if k == 0 and (started or t):
                    pe.wait_ge(att_sb, TPC * i + t)
                for j in range(HPH // 2):
                    pair = k * HPH // 2 + j
                    for w in range(NW):
                        last = pe.matmul(
                            o_bank[WINDOW * w:WINDOW * (w + 1), pair * 2 * VW:(pair + 1) * 2 * VW],
                            probsT[u % 2][:, j * P + WINDOW * w:j * P + WINDOW * (w + 1)],
                            v_pairs[:, t, w, pair, :, :].rearrange("p h v -> p (h v)"), start=True, stop=True)
                last.then_inc(pv_ps, 1)

            def cross_turn(c):
                pe.wait_ge(x1n_sb, TPC * (c + 1))
                turn(g_bank[1], x1n, x1nT_ps)

            def cross_gate(c, bank):
                features(bank, wg, 0, x1nT, w_ps)

            def cross_queries(c, bank):
                for h in range(KT):
                    dst = bank[:, h * TOK:(h + 1) * TOK]
                    pe.matmul(dst, gram[0][:, h, :], x1nT[0][:, h, :], start=True, stop=False)
                    pe.matmul(dst, gram[1][:, h, :], x1nT[0][:, h, :], start=False, stop=False)
                    last = pe.matmul(dst, gram[0][:, h, :], x1nT[1][:, h, :], start=False, stop=True)
                last.then_inc(qp_ps, 1)

            def cross_scores(c, src):
                pe.wait_ge(qp_sb, c + 1)
                if src is ctxT:
                    pe.wait_ge(ld_ctx, 16 * (c + 1))
                for t in range(TPC):
                    for h in range(KT):
                        last = pe.matmul(c_bank[:, h * P:(h + 1) * P], src[:, h, t * P:(t + 1) * P],
                                         qpT[:, h, t * P:(t + 1) * P], start=False, stop=True,
                                         skip_group_check=True)
                last.then_inc(sc_ps, 1)

            def cross_values(src, bank):
                for h in range(KT):
                    for t in range(TPC):
                        last = pe.matmul(bank[:, h * TOK + t * P:h * TOK + (t + 1) * P],
                                         src[:, h, t * P:(t + 1) * P], wh_sb[:, h, :], start=True, stop=True)
                last.then_inc(vx_ps, 1)

            def attention(i, first, last):
                started = not first
                scores(i, 0, started)
                scores(i, 1, started)
                if not last:
                    pe.wait_ge(hn_sb, TPC * (i + 2))
                    if first:
                        pe.wait_ge(gram_sb_done, 1)
                    elif type(i) is not int or i > 1:
                        pe.wait_ge(vx_sb, i - 1)
                    turn(g_bank[0], hn, hT_ps)
                scores(i, 2, started)
                turn_probs(i, 0, started)
                scores(i, 3, started)
                if not last:
                    pe.wait_ge(hT_hi, i + 2)
                    if first:
                        pe.wait_ge(v_sb, 1)
                    else:
                        pe.wait_ge(x1_sb, i)
                    features(g_bank[1], wqkv, D, hT, k_ps, (hT_lo, i + 2))
                values(i, 0, started)
                turn_probs(i, 1, started)
                if not last:
                    features(g_bank[0], wqkv, 0, hT, q_ps)
                turn_probs(i, 2, started)
                values(i, 1, started)
                if not first:
                    if last:
                        pe.wait_ge(x1_sb, i)
                    else:
                        pe.wait_ge(k_sb, i + 2)
                    cross_turn(i - 1)
                turn_probs(i, 3, started)
                if not last:
                    pe.wait_ge(q_sb, i + 2)
                    tokens(g_bank[0], hT, wqkv, 2 * D, v_ps)
                values(i, 2, started)
                values(i, 3, started)
                if not first:
                    pe.wait_ge(x1nT_lo, i)
                    if not last:
                        cross_gate(i - 1, g_bank[1])
                    pe.wait_ge(pT_sb, UNITS * (i + 1) - 1)
                    cross_queries(i - 1, t_bank[0])
                if not last:
                    pe.wait_ge(v_sb, i + 2)
                else:
                    pe.wait_ge(vx_sb, i - 1)
                pe.wait_ge(att_sb, TPC * (i + 1))
                turn(g_bank[0], att, attT_ps)
                if first:
                    pe.wait_ge(wag_lo, 1)
                    pe.wait_ge(k_sb, i + 2)
                else:
                    cross_scores(i - 1, ctxT)
                    if last:
                        pe.wait_ge(sub_sb, UNITS * (i + 1))
                    else:
                        pe.wait_ge(w_sb, i)
                pe.wait_ge(attT_hi, i + 1)
                tokens(s_bank[0] if last else g_bank[1], attT, wout, 0, y_ps, (attT_lo, i + 1))
                if last:
                    cross_gate(i - 1, g_bank[1])
                if not first:
                    cross_values(ctxT, g_bank[0])

            pe.wait_ge(zeros_set, 1)
            for _ in range(WAKE):
                pe.matmul(c_bank[:, 0:KT * P], zeros[:, 0:P], zeros[:, 0:KT * P], start=True, stop=True,
                          skip_group_check=True)
            pe.wait_ge(ld_first, 16)
            pe.wait_ge(hn_sb, TPC)
            turn(g_bank[0], hn, hT_ps)
            pe.wait_ge(wqkv_hi, 1)
            pe.wait_ge(wqkv_lo, 1)
            pe.wait_ge(hT_hi, 1)
            features(g_bank[1], wqkv, D, hT, k_ps, (hT_lo, 1))
            pe.wait_ge(wqkv_lo, 2)
            features(g_bank[0], wqkv, 0, hT, q_ps)
            pe.wait_ge(wqkv_lo, 3)
            pe.wait_ge(k_sb, 1)
            tokens(g_bank[1], hT, wqkv, 2 * D, v_ps)
            pe.wait_ge(ld_const, 16)
            pe.wait_ge(q_sb, 1)
            for h in range(KT):
                mm = pe.matmul(g_bank[0][:, h * P:(h + 1) * P], whT_sb[:, h, :], whT_sb[:, h, :], start=True, stop=True)
            mm.then_inc(gram_ps, 1)
            pe.wait_ge(pool_const, 3)
            pe.wait_ge(ld_mask, 16)

            attention(0, True, False)
            pe.wait_ge(wag_lo, 2)
            pe.wait_ge(gram_lo, 1)
            attention(1, False, False)
            with pe.Fori(2, NC - 1) as i:
                attention(i, False, False)
            attention(NC - 1, False, True)
            pe.wait_ge(ld_ctx_last, 16)
            cross_values(ctxT_last, t_bank[1])
            pe.wait_ge(w_sb, NC - 1)
            cross_turn(NC - 1)
            pe.wait_ge(x1nT_hi, NC)
            pe.wait_ge(x1nT_lo, NC)
            cross_queries(NC - 1, s_bank[1])
            cross_scores(NC - 1, ctxT_last)
            pe.wait_ge(vx_sb, NC - 1)
            cross_gate(NC - 1, g_bank[0])

            def cross_out(c, bank=o_bank):
                if type(c) is not int or c > 1:
                    pe.wait_ge(on_sb, TPC * c)
                for h in range(KT):
                    mm = pe.matmul(bank[:, :].rearrange("p (t h e) -> p t h e", t=TPC, h=KT)[:, :, h, :],
                                   aT[:, h, :], v_all[:, h, c, :], start=True, stop=True)
                mm.then_inc(o_ps, 1)

            def norm_turn(c):
                pe.wait_ge(on_sb, TPC * (c + 1))
                if type(c) is not int or c > 0:
                    pe.wait_ge(yT_sb, KT * c)
                turn(t_bank[0], on, yT_ps)

            def second(j, head, tail, turns, more):
                if head:
                    pe.wait_ge(x2n_sb, TPC * j)
                    if type(j) is not int or j > 1:
                        pe.wait_ge(x2nT_lo, j - 1)
                    turn(t_bank[1], x2n, x2nT_ps)
                if tail:
                    pe.wait_ge(zT_hi, j + 1)
                    if type(j) is not int or j > 0:
                        pe.wait_ge(x2_sb, j)
                    tokens(g_bank[1], zT, wo, 0, z_ps, (zT_lo, j + 1))
                if head:
                    pe.wait_ge(x2nT_hi, j)
                    if type(j) is not int or j > 1:
                        pe.wait_ge(uT_lo, j - 1)
                    features(s_bank[0], wup, 0, x2nT, up_ps, (x2nT_lo, j))
                if turns:
                    norm_turn(j + 1)
                if head:
                    if type(j) is not int or j > 1:
                        pe.wait_ge(moe_sb, TPC * (j - 1))
                    for t, bank in enumerate(EX_BANKS):
                        mm = rows_by(bank[:, 0:D + E], x2nT, wex, t, D + E, 0)
                    mm.then_inc(ex_ps, 1)
                if more:
                    cross_out(j + 2)
                if head:
                    pe.wait_ge(uT_hi, j)
                    if type(j) is not int or j > 1:
                        pe.wait_ge(out_sb, j - 1)
                    tokens(c_bank, uT, wdn, 0, dn_ps, (uT_lo, j))

            pe.wait_ge(aT_sb, 1)
            pe.wait_ge(later_lo, STEPS)
            cross_out(0)
            cross_out(1, t_bank[1])
            norm_turn(0)
            norm_turn(1)
            second(0, False, True, False, True)
            second(1, True, True, True, True)
            with pe.Fori(2, NC - 2) as j:
                second(j, True, True, True, True)
            second(NC - 2, True, True, True, False)
            second(NC - 1, True, True, False, False)
            second(NC, True, False, False, False)


def kernel(**inputs):
    import ml_dtypes
    import numpy as np
    import concourse.bacc as _bacc
    from concourse import mybir as _mybir
    from concourse.bass_utils import run_bass_kernel_spmd as _run

    a = {n: np.ascontiguousarray(v) for n, v in inputs.items()}
    b_qkv = a["L0_attn_b_qkv"]
    d = b_qkv.size // 3
    b, s = a["x"].shape[:2]
    kt = d // P
    tpc = 2

    window = 64
    mask = np.zeros((P, P + window), ml_dtypes.bfloat16)
    mask[np.arange(P) % window, np.arange(P)] = 1
    mask[:window, P:][np.triu_indices(window, 1)] = -1e30
    heads, hd = a["L0_xattn_Wh"].shape[:2]
    gam = (1.0 - 2.0 ** (-5.0 - np.arange(heads))).astype(np.float32)
    idx = np.arange(s, dtype=np.float32)
    expo = idx[None, :] - idx[:, None]
    dm = np.where(expo[None] <= 0, gam[:, None, None] ** expo[None], np.float32(0)).astype(np.float32)
    dm = dm / np.sqrt(dm.sum(axis=-1))[:, None, :]
    decay = (dm / np.sqrt(np.float32(hd))).transpose(2, 0, 1).reshape(P, -1).astype(np.float32)

    def by_half(w):
        return w.reshape(kt, P, -1).transpose(1, 0, 2).reshape(P, -1)

    def columns(v):
        return v.reshape(-1, P).T

    def rows(v):
        return np.broadcast_to(v, (P, v.size))

    wh = a["L0_xattn_Wh"]
    wex = np.concatenate([a["L0_ffn_W_expert"], a["L0_ffn_W_gate"].T], axis=1)
    arrays = {
        "x": a["x"],
        "ctx": a["ctx_2048"].reshape(b // tpc, tpc, s, kt, P).transpose(0, 4, 3, 1, 2).reshape(b // tpc, P, kt, tpc * s),
        "first": np.concatenate([np.eye(P, dtype=np.float32), columns(b_qkv[:2 * d]),
                                 np.repeat(np.eye(P // 16, dtype=np.float32), 16, axis=0)], axis=1),
        "w_qkv": a["L0_attn_W_qkv"],
        "const": np.concatenate([
            rows(b_qkv[2 * d:]), rows(a["L0_attn_b_out"]), decay,
            wh.transpose(1, 0, 2).reshape(P, -1), wh.transpose(2, 0, 1).reshape(P, -1),
            columns(a["L0_xattn_gn_gamma"]), columns(a["L0_xattn_gn_beta"])], axis=1),
        "weights": np.concatenate([by_half(w) for w in (
            a["L0_attn_W_out"], a["L0_xattn_wg_w"], a["L0_xattn_wo_w"], a["L0_ffn_W_up"].T, a["L0_ffn_W_down"].T,
            wex)], axis=1),
        "mask": mask,
    }
    arrays = {f"in_{n}_dram": np.ascontiguousarray(v) for n, v in arrays.items()}
    nc = _bacc.Bacc("TRN2", target_bir_lowering=False, num_devices=1)
    args = [nc.dram_tensor(n, v.shape, _mybir.dt.from_np(v.dtype), kind="ExternalInput").ap()
            for n, v in arrays.items()]
    args.append(nc.dram_tensor("out_0_dram", a["x"].shape, _mybir.dt.from_np(a["x"].dtype),
                               kind="ExternalOutput").ap())
    bass_decoder_layer_kernel(nc, *args)
    r = _run(nc, [arrays], core_ids=[0])
    return r.results[0]["out_0_dram"]
```

```python
from contextlib import ExitStack

import concourse.bass as bass
from concourse import mybir

ALU = mybir.AluOpType
ACT = mybir.ActivationFunctionType
F32 = mybir.dt.float32
F32R = mybir.dt.float32r
BF16 = mybir.dt.bfloat16
AX_X = mybir.AxisListType.X

P = 128
LN_EPS = 1e-5
GN_EPS = 1e-3
WINDOW = 64
HEADS = 16
DH = 16
ATT_SCALE = float(DH) ** -0.5


def bass_decoder_layer_kernel(nc, x, ctx_in, first_in, w_qkv, const_in, weights_in, mask_in, out):
    B, S, D = x.shape
    KT = D // P
    TPC = 2
    NC = B // TPC
    TOK = TPC * P
    NW = S // WINDOW
    HPH = HEADS // KT
    PAIRS = HEADS // 2
    VW = DH + 1
    W2 = KT * D
    E = weights_in.shape[1] // KT - 6 * D
    W_EX = KT * (D + E)
    STEPS = NC - 2
    PART = (3 * W2 + W_EX) // STEPS
    assert S == P and D == 2 * P and NW == 2 and PART * STEPS == 3 * W2 + W_EX

    with ExitStack() as ctx:
        def sb(name, shape, dt=F32):
            return ctx.enter_context(nc.sbuf_tensor(name, shape, dt))

        def pb(name):
            return ctx.enter_context(nc.psum_tensor(name, [P, 512], F32))

        def sem(name):
            return ctx.enter_context(nc.semaphore(name))

        def pair(name, shape):
            return sb(name + "_hi", shape, F32R), sb(name + "_lo", shape, F32R)

        x_all = sb("x_all", [P, NC, TPC * D])
        v_all = sb("v_all", [P, NC, KT, TOK])
        wT_all = sb("wT_all", [P, KT, NC, TOK])
        first_sb = sb("first_sb", [P, P + 2 * KT + HPH])
        wqkv_raw = sb("wqkv_raw", [P, KT, 3 * D])
        wqkv = pair("wqkv", [P, KT, 3 * D])
        const_sb = sb("const_sb", list(const_in.shape))
        w_raw = sb("w_raw", [P, 2 * W2 + STEPS * PART])
        wag = pair("wag", [P, 2, KT, D])
        later = pair("later", [P, STEPS, PART])
        gram_sb = sb("gram_sb", [P, KT, P])
        gram = pair("gram", [P, KT, P])
        mask_sb = sb("mask_sb", [P, P + WINDOW], BF16)
        zeros = sb("zeros", [P, 2 * P], BF16)
        minus_half, minus_one, ln_eps, gn_eps = (
            sb(n, [P, TPC]) for n in ("minus_half", "minus_one", "ln_eps", "gn_eps"))
        hn = sb("hn", [P, TPC, D])
        hT = pair("hT", [P, KT, TOK])
        kT = sb("kT", [P, KT, TOK])
        qT = sb("qT", [P, KT, TOK])
        k_heads = sb("k_heads", [P, KT, HPH, TOK])
        v_pairs = sb("v_pairs", [P, TPC, NW, PAIRS, 2, VW])
        probs = [sb(f"probs{n}", [P, HPH, WINDOW]) for n in range(2)]
        probsT = [sb(f"probsT{n}", [P, 512]) for n in range(2)]
        rowmax = sb("rowmax", [P, 2, HPH])
        rsum = sb("rsum", [P, TPC, HEADS])
        att = sb("att", [P, TPC, D])
        attT = pair("attT", [P, KT, TOK])
        x1n = sb("x1n", [P, TPC, D])
        x1nT = pair("x1nT", [P, KT, TOK])
        qpT = sb("qpT", [P, KT, TOK])
        ctxT = sb("ctxT", [P, KT, TOK])
        bn1, bn2 = (sb(f"bn{n}", [P, TPC, 6]) for n in (1, 2))
        mv1, mv2 = (sb(f"mv{n}", [P, TPC, 2]) for n in (1, 2))
        rs1, rs2 = (sb(f"rs{n}", [P, TPC]) for n in (1, 2))
        ve1, ve2 = (sb(f"ve{n}", [P, TPC]) for n in (1, 2))
        def norm_set(m):
            return tuple(sb(f"{n}{m}", [P, TPC, w] if w else [P, TPC]) for n, w in
                         (("bn", 6), ("mv", 2), ("ve", 0), ("rs", 0), ("neg_mean", 0), ("shift", 0)))

        norm_o = norm_set("_o0"), norm_set("_o1")
        norm_x2 = norm_set("_x2")
        dec = sb("dec", [P, KT * P])
        dabs = sb("dabs", [P, KT * P])
        exp_warm = sb("exp_warm", [P, 1])
        mask_full = sb("mask_full", [P, HPH * WINDOW])
        aT = sb("aT", [P, KT, P])
        on = sb("on", [P, TPC, D])
        yT = sb("yT", [P, KT, TOK])
        z_full = sb("z_full", [P, KT, TOK])
        zT = pair("zT", [P, KT, TOK])
        x2n = sb("x2n", [P, TPC, D])
        x2nT = pair("x2nT", [P, KT, TOK])
        uT = pair("uT", [P, KT, TOK])
        moe = sb("moe", [P, TPC, D])
        top = sb("top", [P, TPC, 8])
        ldiff, esec, eden, einv, rw = (sb(n, [P, TPC]) for n in ("ldiff", "esec", "eden", "einv", "rw"))

        ident = first_sb[:, 0:P]
        bqk_sb = first_sb[:, P:P + 2 * KT]
        head_rows = first_sb[:, P + 2 * KT:P + 2 * KT + HPH]
        bv_sb = const_sb[:, 0:D]
        bout_sb = const_sb[:, D:2 * D]
        decay = const_sb[:, 2 * D:2 * D + KT * P]
        wh_sb = const_sb[:, 3 * D:4 * D].rearrange("p (h e) -> p h e", h=KT)
        whT_sb = const_sb[:, 4 * D:5 * D].rearrange("p (h e) -> p h e", h=KT)
        gb_sb = const_sb[:, 5 * D:5 * D + 2 * KT]
        mask_sel = mask_sb[:, 0:P]
        mask = mask_sb[:, P:P + WINDOW]

        def part_of(packed, first, width):
            return tuple(p.rearrange("p a b -> p (a b)")[:, first:first + KT * width]
                         .rearrange("p (k n) -> p k n", k=KT) for p in (packed[0][:, :, :], packed[1][:, :, :]))

        wout = tuple(p[:, 0] for p in wag)
        wg = tuple(p[:, 1] for p in wag)
        wo = part_of(later, 0, D)
        wup = part_of(later, W2, D)
        wdn = part_of(later, 2 * W2, D)
        wex = part_of(later, 3 * W2, D + E)

        s_bank = [pb("s_bank0"), pb("s_bank1")]
        t_bank = [pb("t_bank0"), pb("t_bank1")]
        o_bank = pb("o_bank")
        g_bank = [pb("g_bank0"), pb("g_bank1")]
        c_bank = pb("c_bank")

        ld_x0, ld_x1, ld_x, ld_ctx, ld_ctx_all, ld_first, ld_wqkv, ld_mask, ld_const, ld_wag, ld_w = map(
            sem, "ld_x0 ld_x1 ld_x ld_ctx ld_ctx_all ld_first ld_wqkv ld_mask ld_const ld_wag ld_w".split())
        zeros_set, small_set, pool_const, first_keys = map(sem, "zeros_set small_set pool_const first_keys".split())
        wqkv_hi, wqkv_lo, wag_hi, wag_lo, later_hi, later_lo = map(
            sem, "wqkv_hi wqkv_lo wag_hi wag_lo later_hi later_lo".split())
        gram_ps, gram_sb_done, gram_hi, gram_lo = map(sem, "gram_ps gram_sb_done gram_hi gram_lo".split())
        hT_ps, k_ps, q_ps, v_ps, attT_ps, y_ps = map(sem, "hT_ps k_ps q_ps v_ps attT_ps y_ps".split())
        x1nT_ps, w_ps, qp_ps, vx_ps, sc_ps = map(sem, "x1nT_ps w_ps qp_ps vx_ps sc_ps".split())
        s_ps, pT_ps, pv_ps = map(sem, "s_ps pT_ps pv_ps".split())
        k_sb, q_sb, v_sb, x1_sb, w_sb, qp_sb, vx_sb = map(sem, "k_sb q_sb v_sb x1_sb w_sb qp_sb vx_sb".split())
        hT_hi, hT_lo, attT_hi, attT_lo, x1nT_hi, x1nT_lo = map(
            sem, "hT_hi hT_lo attT_hi attT_lo x1nT_hi x1nT_lo".split())
        max_sb, sub_sb, exp_sb, pT_sb, rsum_sb, att_sb = map(sem, "max_sb sub_sb exp_sb pT_sb rsum_sb att_sb".split())
        kh_dma = sem("kh_dma")
        ag1, pe1, ps1, hn_sb, xb_sb = map(sem, "ag1 pe1 ps1 hn_sb xb_sb".split())
        ag2, pe2, ps2, x1n_sb = map(sem, "ag2 pe2 ps2 x1n_sb".split())
        ag3, nm3, pe3, ps3, sh3, on_sb, on1_sb = map(sem, "ag3 nm3 pe3 ps3 sh3 on_sb on1_sb".split())
        ag4, nm4, pe4, ps4, sh4, x2n0_sb, x2n1_sb = map(sem, "ag4 nm4 pe4 ps4 sh4 x2n0_sb x2n1_sb".split())
        dec_sb, abs_sb, aT_sb = map(sem, "dec_sb abs_sb aT_sb".split())
        o_ps, yT_ps, z_ps, x2nT_ps, up_ps, ex_ps, dn_ps = map(sem, "o_ps yT_ps z_ps x2nT_ps up_ps ex_ps dn_ps".split())
        yT_sb, z0_sb, z1_sb, zT_hi, zT_lo, x2_sb = map(sem, "yT_sb z0_sb z1_sb zT_hi zT_lo x2_sb".split())
        x2nT_hi, x2nT_lo, uT_hi, uT_lo = map(sem, "x2nT_hi x2nT_lo uT_hi uT_lo".split())
        top_sb, ld_sb, es_sb, ed_sb, ei_sb, rw_sb, moe_sb, dn_sb, out_sb = map(
            sem, "top_sb ld_sb es_sb ed_sb ei_sb rw_sb moe_sb dn_sb out_sb".split())
        st_out = sem("st_out")
        mask_ps, mask_full_sb, mask_laid = map(sem, "mask_ps mask_full_sb mask_laid".split())

        out_dram = out.rearrange("(c t) s d -> s c t d", t=TPC)
        x_dram = x.rearrange("(c t) s d -> s c t d", t=TPC)

        def tiles(ap):
            return ap.rearrange("p (t d) -> p t d", t=TPC)

        def halves(bank, n=512):
            return bank[:, 0:n].rearrange("p (k n) -> p k n", k=KT)

        def down_bank(c):
            return o_bank if type(c) is int and c in (NC - 3, NC - 1) else c_bank

        def z_of(c):
            if type(c) is int and c == 1:
                return moe[:, :, :], uT
            return z_full[:, :, :], zT

        def gate(engine, c, k):
            full, _ = z_of(c)
            if type(c) is not int or c > 2:
                engine.wait_ge(zT_lo, c)
            elif c == 2:
                engine.wait_ge(zT_lo, 1)
            if type(c) is int and c == 1:
                full = full.rearrange("p t d -> p (t d)").rearrange("p (k n) -> p k n", k=KT)
            engine.wait_ge(yT_sb, KT * c + k + 1)
            engine.tensor_tensor(full[:, k, :], yT[:, k, :], wT_all[:, k, c, :], ALU.mult).then_inc((z0_sb, z1_sb)[k], 1)

        UNITS = TPC * KT
        NK = HPH
        VX_BANKS = [g_bank[0], t_bank[1], g_bank[0], t_bank[1], g_bank[0], g_bank[0], s_bank[1], g_bank[1]]
        WAKE = 26
        DVE_BLOCKS, ACT_BLOCKS, POOL_BLOCKS = range(0, 5), range(5, 7), range(7, 8)
        EX_BANKS = (s_bank[1], g_bank[0])

        block = ctx.enter_context(nc.Block())

        @block.sync
        def _(sp):
            sp.dma_start(tiles(x_all[:, 0, :]), x_dram[:, 0]).then_inc(ld_x0, 16)
            sp.dma_start(wqkv_raw[:, :, :], w_qkv.rearrange("(k p) n -> p k n", p=P)).then_inc(ld_wqkv, 16)
            sp.dma_start(tiles(x_all[:, 1, :]), x_dram[:, 1]).then_inc(ld_x1, 16)
            sp.dma_start(mask_sb[:, :], mask_in).then_inc(ld_mask, 16)
            sp.dma_start(w_raw[:, 0:2 * W2], weights_in[:, 0:2 * W2]).then_inc(ld_wag, 16)
            sp.dma_start(x_all[:, 2:NC, :].rearrange("p c (t d) -> p c t d", t=TPC), x_dram[:, 2:NC]).then_inc(ld_x, 16)
            sp.dma_start(ctxT[:, :, :], ctx_in[0]).then_inc(ld_ctx, 16)

            def spread_keys(c):
                sp.wait_ge(k_sb, c + 1)
                sp.wait_ge(s_ps, UNITS * c)
                for h in range(HPH):
                    rows = slice(DH * h, DH * h + DH)
                    sp.dma_start(k_heads[rows, :, h, :], kT[rows, :, :]).then_inc(kh_dma, 16)

            sp.wait_ge(first_keys, HPH)
            spread_keys(1)
            sp.dma_start(w_raw[:, 2 * W2:], weights_in[:, 2 * W2:]).then_inc(ld_w, 16)
            sp.dma_start(v_all[:, :, :, :], ctx_in.rearrange("c p k n -> p c k n")).then_inc(ld_ctx_all, 16)
            with sp.Fori(1, NC - 1) as c:
                spread_keys(c + 1)
                sp.wait_ge(sc_ps, c)
                sp.dma_start(ctxT[:, :, :], ctx_in[c]).then_inc(ld_ctx, 16)
            with sp.Fori(0, NC - 1) as c:
                sp.wait_ge(out_sb, c + 1)
                sp.dma_start(out_dram[:, c], tiles(x_all[:, c, :])).then_inc(st_out, 16)
            for t in range(TPC):
                sp.wait_ge(out_sb, NC + t)
                sp.dma_start(out_dram[:, NC - 1, t, :], x_all[:, NC - 1, t * D:(t + 1) * D]).then_inc(st_out, 16)
            sp.wait_ge(st_out, 16 * (NC - 1 + TPC))

        @block.gpsimd
        def _(pool):
            pool.memset(zeros[:, :], 0.0).then_inc(zeros_set, 1)
            pool.memset(minus_half[:, :], -0.5)
            pool.memset(minus_one[:, :], -1.0)
            pool.memset(ln_eps[:, :], LN_EPS)
            pool.memset(gn_eps[:, :], GN_EPS).then_inc(small_set, 1)
            pool.wait_ge(small_set, 1)

            def rsqrt(c, mv, ve, rs, ag, pe, ps, eps):
                pool.wait_ge(ag, TPC * (c + 1))
                pool.tensor_tensor(ve[:, :], mv[:, :, 1], eps[:, :], ALU.add).then_inc(pe, 1)
                pool.wait_ge(pe, c + 1)
                pool.tensor_tensor(rs[:, :], ve[:, :], minus_half[:, :], ALU.pow).then_inc(ps, 1)

            def norm1(c):
                rsqrt(c, mv1, ve1, rs1, ag1, pe1, ps1, ln_eps)

            def add_bias(c):
                pool.wait_ge(hn_sb, TPC * (c + 1))
                for t in range(TPC):
                    xt = x_all[:, c, t * D:(t + 1) * D]
                    pool.tensor_tensor(xt, xt, bout_sb, ALU.add).then_inc(xb_sb, 1)

            def split_later(s):
                pool.wait_ge(ld_w, 16)
                raw = w_raw[:, 2 * W2:].rearrange("p (a b) -> p a b", b=PART)[:, s, :]
                pool.tensor_copy(later[0][:, s, :], raw).then_inc(later_hi, 1)
                pool.wait_ge(later_hi, s + 1)
                pool.tensor_tensor(later[1][:, s, :], raw, later[0][:, s, :].bitcast(F32),
                                   ALU.subtract).then_inc(later_lo, 1)

            norm1(0)
            pool.memset(v_pairs[:, :, :, :, :, :], 0.0).then_inc(pool_const, 1)
            pool.wait_ge(pool_const, 1)
            for h in range(2):
                rows = slice(WINDOW * h, WINDOW * h + WINDOW)
                pool.memset(v_pairs[rows, :, :, :, h, DH:VW], 1.0).then_inc(pool_const, 1)
                pool.wait_ge(pool_const, 2 + h)
            pool.wait_ge(ld_first, 16)
            pool.wait_ge(k_sb, 1)
            for h in POOL_BLOCKS:
                pool.tensor_tensor(k_heads[:, :, h, :], kT[:, :, :],
                                   head_rows[:, h:h + 1].unsqueeze(2).broadcast_to([P, KT, TOK]),
                                   ALU.mult).then_inc(first_keys, 1)
            norm1(1)
            pool.wait_ge(ld_wag, 16)

            def split_wag(m):
                raw = w_raw[:, m * W2:(m + 1) * W2].rearrange("p (k n) -> p k n", k=KT)
                pool.tensor_copy(wag[0][:, m], raw).then_inc(wag_hi, 1)
                pool.wait_ge(wag_hi, m + 1)
                pool.tensor_tensor(wag[1][:, m], raw, wag[0][:, m].bitcast(F32), ALU.subtract).then_inc(wag_lo, 1)

            split_wag(0)
            split_wag(1)
            pool.wait_ge(ld_const, 16)
            add_bias(0)
            add_bias(1)

            def attention(i, first, more):
                if more:
                    norm1(i + 2)
                if first:
                    pool.wait_ge(gram_sb_done, 1)
                    pool.tensor_copy(gram[0][:, :, :], gram_sb[:, :, :]).then_inc(gram_hi, 1)
                    pool.wait_ge(gram_hi, 1)
                    pool.tensor_tensor(gram[1][:, :, :], gram_sb[:, :, :], gram[0][:, :, :].bitcast(F32),
                                       ALU.subtract).then_inc(gram_lo, 1)
                if more:
                    split_later(i)
                    add_bias(i + 2)
                rsqrt(i, mv2, ve2, rs2, ag2, pe2, ps2, ln_eps)

            attention(0, True, True)
            with pool.Fori(1, NC - 2) as i:
                attention(i, False, True)
            attention(NC - 2, False, False)
            attention(NC - 1, False, False)

            def scale_and_shift(c, tensors, ag, nm, pe, ps, sh, eps):
                _, mv, ve, rs, neg_mean, shift = tensors
                pool.wait_ge(ag, TPC * (c + 1))
                if type(c) is not int or c > 0:
                    pool.wait_ge(sh, c)
                pool.tensor_tensor(neg_mean[:, :], mv[:, :, 0], minus_one[:, :], ALU.mult).then_inc(nm, 1)
                rsqrt(c, mv, ve, rs, ag, pe, ps, eps)
                pool.wait_ge(nm, c + 1)
                pool.wait_ge(ps, c + 1)
                pool.tensor_tensor(shift[:, :], neg_mean[:, :], rs[:, :], ALU.mult).then_inc(sh, 1)

            def norm3(c, which=0):
                scale_and_shift(c, norm_o[which], ag3, nm3, pe3, ps3, sh3, gn_eps)

            def z_lo(c):
                full, parts = z_of(c)
                pool.wait_ge(zT_hi, c + 1)
                pool.tensor_tensor(parts[1][:, :, :], full, parts[0][:, :, :].bitcast(F32),
                                   ALU.subtract).then_inc(zT_lo, 1)

            def norm4(c):
                if type(c) is not int or c > 0:
                    pool.wait_ge(x2n0_sb, c)
                    pool.wait_ge(x2n1_sb, c)
                scale_and_shift(c, norm_x2, ag4, nm4, pe4, ps4, sh4, ln_eps)

            def add_moe(c):
                pool.wait_ge(moe_sb, TPC * (c + 1))
                pool.wait_ge(dn_sb, c + 1)
                pool.tensor_tensor(x_all[:, c, :], x_all[:, c, :], moe[:, :, :].rearrange("p t d -> p (t d)"),
                                   ALU.add).then_inc(out_sb, 1)

            norm3(0)
            norm3(1, 1)
            gate(pool, 0, 0)
            z_lo(0)
            norm3(2)
            z_lo(1)
            norm4(0)
            norm4(1)
            norm3(3)
            with pool.Fori(2, NC - 2) as j:
                norm4(j)
                gate(pool, j + 1, 0)
                add_moe(j - 2)
                norm3(j + 2)
            norm4(NC - 2)
            add_moe(NC - 4)
            norm4(NC - 1)
            add_moe(NC - 3)
            add_moe(NC - 2)

        @block.scalar
        def _(act):
            act.dma_start(first_sb[:, :], first_in).then_inc(ld_first, 16)
            act.dma_start(const_sb[:, :], const_in).then_inc(ld_const, 16)

            def copy_out(c, filled, bank, dst, done):
                act.wait_ge(filled, c + 1)
                act.activation(dst, halves(bank), ACT.Copy).then_inc(done, 1)

            def hT_out(c):
                copy_out(c, hT_ps, g_bank[0], hT[0][:, :, :], hT_hi)

            def k_out(c, bank):
                act.wait_ge(k_ps, c + 1)
                for k in range(KT):
                    last = act.activation(kT[:, k, :], halves(bank)[:, k, :], ACT.Identity,
                                          bias=bqk_sb[:, KT + k:KT + k + 1])
                last.then_inc(k_sb, 1)

            def q_out(c, bank):
                act.wait_ge(q_ps, c + 1)
                for k in range(KT):
                    last = act.activation(qT[:, k, :], halves(bank)[:, k, :], ACT.Identity,
                                          bias=bqk_sb[:, k:k + 1])
                last.then_inc(q_sb, 1)

            def exps(i, u):
                act.wait_ge(sub_sb, UNITS * i + u + 1)
                p = probs[u % 2]
                act.activation(p[:, :, :], p[:, :, :], ACT.Exp, scale=ATT_SCALE).then_inc(exp_sb, 1)

            def lay_mask(i, u):
                act.wait_ge(sub_sb, UNITS * i + u - 1)
                act.activation(s_bank[u % 2][:, :], mask_full[:, :], ACT.Copy).then_inc(mask_laid, 1)

            def probsT_out(i, u):
                act.wait_ge(pT_ps, UNITS * i + u + 1)
                act.activation(probsT[u % 2][:, :], t_bank[u % 2][:, :], ACT.Copy).then_inc(pT_sb, 1)

            def gate_out(c, bank):
                act.wait_ge(w_ps, c + 1)
                act.activation(wT_all[:, :, c, :], halves(bank), ACT.Relu).then_inc(w_sb, 1)

            def values_out(c):
                copy_out(c, vx_ps, VX_BANKS[c], v_all[:, c, :, :], vx_sb)

            def attention(i, first, last):
                if not first:
                    lay_mask(i, 2)
                exps(i, 0)
                if not last:
                    hT_out(i + 1)
                if not first:
                    lay_mask(i, 3)
                exps(i, 1)
                probsT_out(i, 0)
                exps(i, 2)
                if not last:
                    k_out(i + 1, c_bank if first else g_bank[1])
                probsT_out(i, 1)
                if not last:
                    lay_mask(i + 1, 0)
                exps(i, 3)
                if not last:
                    act.wait_ge(s_ps, UNITS * (i + 1))
                    q_out(i + 1, g_bank[0])
                probsT_out(i, 2)
                if last:
                    values_out(0)
                if not first:
                    copy_out(i - 1, x1nT_ps, g_bank[1], x1nT[0][:, :, :], x1nT_hi)
                probsT_out(i, 3)
                if not last:
                    lay_mask(i + 1, 1)
                if first:
                    act.wait_ge(gram_ps, 1)
                    act.activation(gram_sb[:, :, :], halves(g_bank[1], KT * P), ACT.Copy).then_inc(gram_sb_done, 1)
                else:
                    copy_out(i - 1, qp_ps, t_bank[0], qpT[:, :, :], qp_sb)
                copy_out(i, attT_ps, s_bank[1] if last else t_bank[1], attT[0][:, :, :], attT_hi)
                if not first:
                    gate_out(i - 1, g_bank[1])

            act.wait_ge(zeros_set, 1)
            act.activation(exp_warm[:, :], zeros[:, 0:1], ACT.Exp)
            act.wait_ge(ld_first, 16)
            act.wait_ge(ld_wqkv, 16)
            for m in (1, 0, 2):
                act.activation(wqkv[0][:, :, m * D:(m + 1) * D], wqkv_raw[:, :, m * D:(m + 1) * D],
                               ACT.Copy).then_inc(wqkv_hi, 1)
                if m == 0:
                    hT_out(0)
            k_out(0, g_bank[1])
            act.wait_ge(k_sb, 1)
            for h in ACT_BLOCKS:
                act.activation(k_heads[:, :, h, :], kT[:, :, :], ACT.Copy,
                               scale=head_rows[:, h:h + 1]).then_inc(first_keys, 1)
            q_out(0, g_bank[0])
            act.wait_ge(mask_ps, 1)
            act.activation(mask_full[:, :], c_bank[:, :], ACT.Copy).then_inc(mask_full_sb, 1)
            act.wait_ge(mask_full_sb, 1)

            attention(0, True, False)
            with act.Fori(1, NC - 1) as i:
                attention(i, False, False)
            attention(NC - 1, False, True)
            values_out(1)
            values_out(2)
            copy_out(NC - 1, x1nT_ps, t_bank[0], x1nT[0][:, :, :], x1nT_hi)
            values_out(3)
            copy_out(NC - 1, qp_ps, s_bank[1], qpT[:, :, :], qp_sb)
            values_out(4)
            gate_out(NC - 1, s_bank[0])

            def y_out(c, bank=t_bank[0], of=range(KT)):
                act.wait_ge(yT_ps, c + 1)
                if type(c) is not int or c > 0:
                    act.wait_ge(z0_sb, c)
                    act.wait_ge(z1_sb, c)
                for k in of:
                    act.activation(yT[:, k, :], halves(bank)[:, k, :], ACT.Identity,
                                   scale=gb_sb[:, k:k + 1], bias=gb_sb[:, KT + k:KT + k + 1]).then_inc(yT_sb, 1)

            def x2n_out(c):
                rs, shift = norm_x2[3], norm_x2[5]
                act.wait_ge(sh4, c + 1)
                if type(c) is not int or c > 0:
                    act.wait_ge(x2nT_ps, c)
                else:
                    act.wait_ge(yT_ps, 2)
                for t in range(1 if type(c) is int and c in (0, 1, NC - 2, NC - 1) else TPC):
                    act.activation(x2n[:, t, :], x_all[:, c, t * D:(t + 1) * D], ACT.Identity,
                                   scale=rs[:, t:t + 1], bias=shift[:, t:t + 1]).then_inc((x2n0_sb, x2n1_sb)[t], 1)

            def on_out(c):
                rs, shift = norm_o[0][3], norm_o[0][5]
                act.wait_ge(sh3, c + 1)
                if type(c) is not int or c > 0:
                    act.wait_ge(yT_ps, c)
                for t in range(TPC):
                    act.activation(on[:, t, :], o_bank[:, t * D:(t + 1) * D], ACT.Identity,
                                   scale=rs[:, t:t + 1], bias=shift[:, t:t + 1]).then_inc(on_sb, 1)

            def z_hi(c):
                full, parts = z_of(c)
                if type(c) is not int or c > 1:
                    act.wait_ge(z_ps, c)
                act.wait_ge(z0_sb, c + 1)
                act.wait_ge(z1_sb, c + 1)
                act.activation(parts[0][:, :, :], full, ACT.Copy).then_inc(zT_hi, 1)

            def x2nT_out(c):
                copy_out(c, x2nT_ps, t_bank[1], x2nT[0][:, :, :], x2nT_hi)

            def u_out(c):
                act.wait_ge(up_ps, c + 1)
                act.activation(uT[0][:, :, :], halves(s_bank[0]), ACT.Relu).then_inc(uT_hi, 1)

            def exp_out(c):
                act.wait_ge(ld_sb, c + 1)
                act.activation(esec[:, :], ldiff[:, :], ACT.Exp).then_inc(es_sb, 1)

            def moe_out(c):
                act.wait_ge(rw_sb, c + 1)
                if type(c) is not int or c > 0:
                    act.wait_ge(out_sb, c)
                for t, bank in enumerate(EX_BANKS):
                    act.activation(moe[:, t, :], bank[:, 0:D], ACT.Copy, scale=rw[:, t:t + 1]).then_inc(moe_sb, 1)

            on_out(0)
            y_out(0)
            z_hi(0)
            y_out(1, s_bank[0])
            z_hi(1)
            on_out(2)
            y_out(2, of=range(0, 1))
            x2n_out(0)
            y_out(2, of=range(1, KT))
            x2nT_out(0)
            z_hi(2)
            u_out(0)
            x2n_out(1)
            exp_out(0)

            def second(j, z_first):
                x2nT_out(j - 1)
                on_out(j + 1)
                moe_out(j - 2)
                u_out(j - 1)
                y_out(j + 1)
                x2n_out(j)
                if z_first:
                    z_hi(j + 1)
                exp_out(j - 1)
                if not z_first:
                    z_hi(j + 1)

            with act.Fori(2, NC - 2) as j:
                second(j, False)
            second(NC - 2, True)
            x2nT_out(NC - 2)
            moe_out(NC - 3)
            u_out(NC - 2)
            x2n_out(NC - 1)
            exp_out(NC - 2)
            x2nT_out(NC - 1)
            moe_out(NC - 2)
            u_out(NC - 1)
            exp_out(NC - 1)

        @block.vector
        def _(dve):
            def norm_stats(c, src, bn, mv, ag, source=None):
                dve.wait_ge(ld_x0, 16)
                if source is not None:
                    dve.wait_ge(source, c + 1)
                for t in range(TPC):
                    dve.bn_stats(bn[:, t, :], src(t))
                dve.drain()
                for t in range(TPC):
                    dve.bn_aggr(mv[:, t, :], bn[:, t, :]).then_inc(ag, 1)

            def normalize(c, src, dst, mv, rs, ps, done):
                dve.wait_ge(ps, c + 1)
                for t in range(TPC):
                    dve.tensor_scalar(dst[:, t, :], src(t), mv[:, t, 0:1], rs[:, t:t + 1],
                                      ALU.subtract, ALU.mult).then_inc(done, 1)

            def x_tile(c):
                return lambda t: x_all[:, c, t * D:(t + 1) * D]

            def lo_out(c, hi_done, bank, parts, done):
                dve.wait_ge(hi_done, c + 1)
                dve.tensor_tensor(parts[1][:, :, :], halves(bank), parts[0][:, :, :].bitcast(F32),
                                  ALU.subtract).then_inc(done, 1)

            def soften(i, u, started):
                bank = s_bank[u % 2][:, :].rearrange("p (h k) -> p h k", h=HPH)
                dve.wait_ge(s_ps, UNITS * i + u + 1)
                dve.tensor_reduce(rowmax[:, u % 2, :], bank, AX_X, ALU.max).then_inc(max_sb, 1)
                dve.wait_ge(max_sb, UNITS * i + u + 1)
                if started or u >= 2:
                    dve.wait_ge(pT_ps, UNITS * i + u - 1)
                dve.tensor_tensor(probs[u % 2][:, :, :], bank,
                                  rowmax[:, u % 2, :].unsqueeze(2).broadcast_to([P, HPH, WINDOW]),
                                  ALU.subtract).then_inc(sub_sb, 1)

            def v_out(c, bank):
                dve.wait_ge(v_ps, c + 1)
                if type(c) is not int or c > 0:
                    dve.wait_ge(pv_ps, UNITS * c)
                src = bank[:, :].rearrange("p (t j h d) -> p t j h d", t=TPC, h=2, d=DH)
                bias = bv_sb.rearrange("p (j h d) -> p j h d", h=2, d=DH)
                for w in range(NW):
                    for h in range(2):
                        wr = slice(WINDOW * w, WINDOW * w + WINDOW)
                        hr = slice(WINDOW * h, WINDOW * h + WINDOW)
                        last = dve.tensor_tensor(
                            v_pairs[hr, :, w, :, h, 0:DH], src[wr, :, :, h, :],
                            bias[wr, :, h, :].unsqueeze(1).broadcast_to([WINDOW, TPC, PAIRS, DH]), ALU.add)
                last.then_inc(v_sb, 1)

            def att_out(i, t):
                o = o_bank[:, 0:HEADS * VW].rearrange("p (h v) -> p h v", v=VW)
                dve.wait_ge(pv_ps, UNITS * i + KT * (t + 1))
                dve.reciprocal(rsum[:, t, :], o[:, :, DH]).then_inc(rsum_sb, 1)
                dve.wait_ge(rsum_sb, TPC * i + t + 1)
                dve.tensor_tensor(att[:, t, :].rearrange("p (h d) -> p h d", d=DH), o[:, :, 0:DH],
                                  rsum[:, t, :].unsqueeze(2).broadcast_to([P, HEADS, DH]),
                                  ALU.mult).then_inc(att_sb, 1)

            def norm1_stats(c):
                norm_stats(c, x_tile(c), bn1, mv1, ag1)

            def norm1(c):
                normalize(c, x_tile(c), hn, mv1, rs1, ps1, hn_sb)

            def norm2(c):
                normalize(c, x_tile(c), x1n, mv2, rs2, ps2, x1n_sb)

            def norm2_stats(c):
                norm_stats(c, x_tile(c), bn2, mv2, ag2, x1_sb)

            def add_attention(c, bank):
                dve.wait_ge(y_ps, c + 1)
                dve.wait_ge(xb_sb, TPC * (c + 1))
                dve.tensor_tensor(x_all[:, c, :], bank[:, :], x_all[:, c, :], ALU.add).then_inc(x1_sb, 1)

            def attention(i, first, more, last):
                soften(i, 0, not first)
                soften(i, 1, not first)
                if not first:
                    add_attention(i - 1, t_bank[0])
                if not last:
                    lo_out(i + 1, hT_hi, g_bank[0], hT, hT_lo)
                if first:
                    dve.wait_ge(ld_const, 16)
                    dve.wait_ge(pool_const, 3)
                    v_out(0, g_bank[1])
                else:
                    norm2_stats(i - 1)
                soften(i, 2, not first)
                soften(i, 3, not first)
                if not first:
                    norm2(i - 1)
                att_out(i, 0)
                if not first:
                    lo_out(i - 1, x1nT_hi, g_bank[1], x1nT, x1nT_lo)
                if first:
                    dve.wait_ge(ld_x, 16)
                if more:
                    norm1_stats(i + 2)
                att_out(i, 1)
                if not last:
                    v_out(i + 1, g_bank[0])
                lo_out(i, attT_hi, s_bank[1] if last else t_bank[1], attT, attT_lo)
                if more:
                    norm1(i + 2)
                if last:
                    add_attention(i, s_bank[0])

            norm1_stats(0)
            norm1(0)
            dve.wait_ge(ld_wqkv, 16)
            for n, m in enumerate((1, 0, 2)):
                dve.wait_ge(wqkv_hi, n + 1)
                at = slice(m * D, (m + 1) * D)
                dve.tensor_tensor(wqkv[1][:, :, at], wqkv_raw[:, :, at], wqkv[0][:, :, at].bitcast(F32),
                                  ALU.subtract).then_inc(wqkv_lo, 1)
                if m == 0:
                    lo_out(0, hT_hi, g_bank[0], hT, hT_lo)
            dve.wait_ge(ld_x1, 16)
            norm1_stats(1)
            dve.wait_ge(ld_first, 16)
            dve.wait_ge(k_sb, 1)
            for h in DVE_BLOCKS:
                dve.tensor_scalar(k_heads[:, :, h, :], kT[:, :, :], head_rows[:, h:h + 1], None,
                                  ALU.mult).then_inc(first_keys, 1)
            norm1(1)
            attention(0, True, True, False)
            with dve.Fori(1, NC - 2) as i:
                attention(i, False, True, False)
            attention(NC - 2, False, False, False)
            attention(NC - 1, False, False, True)
            norm2_stats(NC - 1)
            norm2(NC - 1)
            lo_out(NC - 1, x1nT_hi, t_bank[0], x1nT, x1nT_lo)

            dve.wait_ge(sc_ps, NC)
            dve.tensor_tensor(dec[:, :], c_bank[:, 0:KT * P], decay, ALU.mult).then_inc(dec_sb, 1)
            dve.wait_ge(dec_sb, 1)
            dve.scalar_tensor_tensor(out=dabs[:, :], in0=dec[:, :], scalar=-1.0, in1=dec[:, :],
                                     op0=ALU.mult, op1=ALU.max).then_inc(abs_sb, 1)
            dve.wait_ge(abs_sb, 1)
            dve.tensor_scalar(aT[:, :, :].rearrange("p k n -> p (k n)"), dabs[:, :], 1.0, None,
                              ALU.max).then_inc(aT_sb, 1)

            def o_stats(c, bank, which=0):
                bn, mv = norm_o[which][0:2]
                norm_stats(c, lambda t: bank[:, t * D:(t + 1) * D], bn, mv, ag3, o_ps)

            def x2_out(c, bank):
                dve.wait_ge(z_ps, c + 1)
                dve.tensor_tensor(x_all[:, c, :], bank[:, :], x_all[:, c, :], ALU.add).then_inc(x2_sb, 1)
                norm_stats(c, x_tile(c), norm_x2[0], norm_x2[1], ag4, x2_sb)

            def x2n_out(c):
                dve.wait_ge(ps4, c + 1)
                if type(c) is not int or c > 0:
                    dve.wait_ge(x2nT_ps, c)
                else:
                    dve.wait_ge(yT_ps, 2)
                dve.tensor_scalar(x2n[:, 1, :], x_all[:, c, D:2 * D], norm_x2[1][:, 1, 0:1], norm_x2[3][:, 1:2],
                                  ALU.subtract, ALU.mult).then_inc(x2n1_sb, 1)

            def z_lo(c):
                dve.wait_ge(zT_hi, c + 1)
                dve.tensor_tensor(zT[1][:, :, :], z_full[:, :, :], zT[0][:, :, :].bitcast(F32),
                                  ALU.subtract).then_inc(zT_lo, 1)

            def u_lo(c):
                dve.wait_ge(uT_hi, c + 1)
                dve.scalar_tensor_tensor(out=uT[1][:, :, :], in0=halves(s_bank[0]), scalar=0.0,
                                         in1=uT[0][:, :, :].bitcast(F32), op0=ALU.max,
                                         op1=ALU.subtract).then_inc(uT_lo, 1)

            def route(c):
                dve.wait_ge(ld_x0, 16)
                dve.wait_ge(ex_ps, c + 1)
                for t, bank in enumerate(EX_BANKS):
                    dve.max(top[:, t, :], bank[:, D:D + E]).then_inc(top_sb, 1)
                dve.wait_ge(top_sb, TPC * (c + 1))
                dve.tensor_tensor(ldiff[:, :], top[:, :, 1], top[:, :, 0], ALU.subtract).then_inc(ld_sb, 1)

            def weigh(c):
                dve.wait_ge(es_sb, c + 1)
                dve.tensor_scalar(eden[:, :], esec[:, :], 1.0, None, ALU.add).then_inc(ed_sb, 1)
                dve.wait_ge(ed_sb, c + 1)
                dve.reciprocal(einv[:, :], eden[:, :]).then_inc(ei_sb, 1)
                dve.wait_ge(ei_sb, c + 1)
                for t in range(TPC):
                    last = dve.scalar_tensor_tensor(out=rw[:, t:t + 1], in0=esec[:, t:t + 1], scalar=einv[:, t:t + 1],
                                                    in1=einv[:, t:t + 1], op0=ALU.mult, op1=ALU.add)
                last.then_inc(rw_sb, 1)

            def add_down(c):
                dve.wait_ge(dn_ps, c + 1)
                dve.tensor_tensor(x_all[:, c, :], down_bank(c)[:, :], x_all[:, c, :], ALU.add).then_inc(dn_sb, 1)

            def add_experts(c):
                dve.wait_ge(dn_sb, c + 1)
                dve.wait_ge(rw_sb, c + 1)
                dve.wait_ge(out_sb, c)
                for t, bank in enumerate(EX_BANKS):
                    xt = x_all[:, c, t * D:(t + 1) * D]
                    dve.scalar_tensor_tensor(out=xt, in0=bank[:, 0:D], scalar=rw[:, t:t + 1], in1=xt,
                                             op0=ALU.mult, op1=ALU.add).then_inc(out_sb, 1)

            def second(j, head, tail, more, gated):
                if head:
                    lo_out(j - 1, x2nT_hi, t_bank[1], x2nT, x2nT_lo)
                if not tail:
                    add_down(j - 2)
                if tail:
                    x2_out(j, g_bank[1])
                u_lo(j - 1)
                if tail:
                    add_down(j - 2)
                if gated:
                    gate(dve, j + 1, 1)
                if gated and not more:
                    gate(dve, j + 1, 0)
                    x2n_out(j)
                route(j - 1)
                if tail and not gated:
                    x2n_out(j)
                if more:
                    o_stats(j + 2, o_bank)
                if gated and not more:
                    z_lo(j + 1)
                weigh(j - 1)
                if more:
                    z_lo(j + 1)

            def values_out(c):
                dve.wait_ge(vx_ps, c + 1)
                dve.tensor_copy(v_all[:, c, :, :], halves(VX_BANKS[c])).then_inc(vx_sb, 1)

            o_stats(0, o_bank)
            o_stats(1, t_bank[1], 1)
            values_out(5)
            values_out(6)
            dve.wait_ge(ps3, 2)
            for t in range(TPC):
                dve.tensor_scalar(x2n[:, t, :], t_bank[1][:, t * D:(t + 1) * D], norm_o[1][1][:, t, 0:1],
                                  norm_o[1][3][:, t:t + 1], ALU.subtract, ALU.mult).then_inc(on1_sb, 1)
            gate(dve, 0, 1)
            values_out(7)
            o_stats(2, o_bank)
            gate(dve, 1, 0)
            gate(dve, 1, 1)
            x2_out(0, g_bank[1])
            x2n_out(0)
            dve.wait_ge(sh4, 1)
            x2_out(1, s_bank[1])
            lo_out(0, x2nT_hi, t_bank[1], x2nT, x2nT_lo)
            gate(dve, 2, 0)
            gate(dve, 2, 1)
            o_stats(3, o_bank)
            u_lo(0)
            x2n_out(1)
            z_lo(2)
            route(0)
            weigh(0)
            with dve.Fori(2, NC - 2) as j:
                second(j, True, True, True, True)
            second(NC - 2, True, True, False, True)
            second(NC - 1, True, True, False, False)
            second(NC, True, False, False, False)
            add_down(NC - 1)
            add_experts(NC - 1)

        @block.tensor
        def _(pe):
            def turn(bank, src, done):
                for k in range(KT):
                    for t in range(TPC):
                        last = pe.transpose(bank[:, k * TOK + t * P:k * TOK + t * P + P],
                                            src[:, t, k * P:(k + 1) * P], ident)
                last.then_inc(done, 1)

            def features(bank, w, col, srcT, done, lo=None, of=range(KT)):
                for wn, sn in ((0, 0), (1, 0), (0, 1)):
                    if sn == 1 and lo is not None:
                        pe.wait_ge(*lo)
                    for f in of:
                        for k in range(KT):
                            last = pe.matmul(bank[:, f * TOK:(f + 1) * TOK],
                                             w[wn][:, k, col + f * P:col + (f + 1) * P], srcT[sn][:, k, :],
                                             start=(f == wn == sn == k == 0), stop=(sn == 1 and k == KT - 1),
                                             skip_group_check=True)
                if f == KT - 1:
                    last.then_inc(done, 1)

            def tokens(banks, srcT, w, width, col, done, lo=None):
                for sn, wn in ((0, 0), (0, 1), (1, 0)):
                    if sn == 1 and lo is not None:
                        pe.wait_ge(*lo)
                    for t, (bank, at) in enumerate(banks):
                        for k in range(KT):
                            last = pe.matmul(bank[:, at:at + width], srcT[sn][:, k, t * P:(t + 1) * P],
                                             w[wn][:, k, col:col + width], start=(at == sn == wn == k == 0),
                                             stop=(sn == 1 and k == KT - 1), skip_group_check=True)
                last.then_inc(done, 1)

            def both(bank):
                return (bank, 0), (bank, D)

            def mask_product(bank):
                return pe.matmul(bank[:, :], mask_sel, mask.unsqueeze(1).broadcast_to([P, HPH, WINDOW]),
                                 start=True, stop=False, skip_group_check=True)

            def scores(i, u, started):
                t, k = divmod(u, KT)
                bank = s_bank[u % 2]
                if started:
                    pe.wait_ge(mask_laid, UNITS * i + u - UNITS + 1)
                else:
                    if u >= 2:
                        pe.wait_ge(sub_sb, u - 1)
                    mask_product(bank)
                if u == 0:
                    if started:
                        pe.wait_ge(kh_dma, 16 * NK * i)
                    else:
                        pe.wait_ge(first_keys, HPH)
                    pe.wait_ge(q_sb, i + 1)
                for w in range(NW):
                    at = t * P + w * WINDOW
                    last = pe.matmul(bank[WINDOW * w:WINDOW * (w + 1), :], qT[:, k, at:at + WINDOW],
                                     k_heads[:, k, :, at:at + WINDOW], start=False, stop=True,
                                     skip_group_check=True)
                last.then_inc(s_ps, 1)

            def turn_probs(i, u, started):
                pe.wait_ge(exp_sb, UNITS * i + u + 1)
                if started or u >= 2:
                    pe.wait_ge(pT_sb, UNITS * i + u - 1)
                for j in range(HPH // 2):
                    src = probs[u % 2][:, 2 * j:2 * j + 2, :].rearrange("p h k -> p (h k)")
                    last = pe.transpose(t_bank[u % 2][:, j * P:(j + 1) * P], src, ident)
                last.then_inc(pT_ps, 1)

            def values(i, u, started):
                t, k = divmod(u, KT)
                pe.wait_ge(pT_sb, UNITS * i + u + 1)
                if u == 0:
                    pe.wait_ge(v_sb, i + 1)
                if k == 0 and (started or t):
                    pe.wait_ge(att_sb, TPC * i + t)
                for j in range(HPH // 2):
                    pair = k * HPH // 2 + j
                    for w in range(NW):
                        last = pe.matmul(
                            o_bank[WINDOW * w:WINDOW * (w + 1), pair * 2 * VW:(pair + 1) * 2 * VW],
                            probsT[u % 2][:, j * P + WINDOW * w:j * P + WINDOW * (w + 1)],
                            v_pairs[:, t, w, pair, :, :].rearrange("p h v -> p (h v)"), start=True, stop=True)
                last.then_inc(pv_ps, 1)

            def cross_turn(c):
                pe.wait_ge(x1n_sb, TPC * (c + 1))
                turn(g_bank[1], x1n, x1nT_ps)

            def cross_gate(c, bank, of=range(KT)):
                features(bank, wg, 0, x1nT, w_ps, of=of)

            def cross_queries(c, bank):
                for gn, xn in ((0, 0), (1, 0), (0, 1)):
                    if xn == 1:
                        pe.wait_ge(x1nT_lo, c + 1)
                    for h in range(KT):
                        last = pe.matmul(bank[:, h * TOK:(h + 1) * TOK], gram[gn][:, h, :], x1nT[xn][:, h, :],
                                         start=(gn == xn == h == 0), stop=(xn == 1), skip_group_check=True)
                last.then_inc(qp_ps, 1)

            def cross_scores(c, src, loaded):
                pe.wait_ge(qp_sb, c + 1)
                if loaded is not None:
                    pe.wait_ge(loaded, 16 * (c + 1))
                for t in range(TPC):
                    for h in range(KT):
                        last = pe.matmul(c_bank[:, h * P:(h + 1) * P], src[:, h, t * P:(t + 1) * P],
                                         qpT[:, h, t * P:(t + 1) * P], start=False, stop=True,
                                         skip_group_check=True)
                last.then_inc(sc_ps, 1)

            def cross_values(c):
                if VX_BANKS[c] in VX_BANKS[:c]:
                    pe.wait_ge(vx_sb, max(b for b in range(c) if VX_BANKS[b] is VX_BANKS[c]) + 1)
                for h in range(KT):
                    for t in range(TPC):
                        last = pe.matmul(VX_BANKS[c][:, h * TOK + t * P:h * TOK + (t + 1) * P],
                                         v_all[:, c, h, t * P:(t + 1) * P], wh_sb[:, h, :], start=True, stop=True)
                last.then_inc(vx_ps, 1)

            def stay_awake(products):
                for _ in range(products):
                    pe.matmul(c_bank[:, 0:KT * P], zeros[:, 0:P], zeros[:, 0:KT * P], start=True, stop=True,
                              skip_group_check=True)

            def attention(i, first, last):
                started = not first
                if not last:
                    pe.wait_ge(hn_sb, TPC * (i + 2))
                    if first:
                        pe.wait_ge(q_sb, 1)
                    else:
                        pe.wait_ge(v_sb, i + 1)
                    turn(g_bank[0], hn, hT_ps)
                if type(i) is not int or i > 1:
                    cross_scores(i - 2, ctxT[:, :, :], ld_ctx)
                scores(i, 2, started)
                if not first:
                    pe.wait_ge(x1_sb, i)
                turn_probs(i, 0, started)
                scores(i, 3, started)
                if not last:
                    pe.wait_ge(hT_hi, i + 2)
                    if first:
                        pe.wait_ge(mask_full_sb, 1)
                    elif type(i) is not int or i > 1:
                        pe.wait_ge(w_sb, i - 1)
                    features(c_bank if first else g_bank[1], wqkv, D, hT, k_ps, (hT_lo, i + 2))
                values(i, 0, started)
                turn_probs(i, 1, started)
                if last:
                    pe.wait_ge(ld_ctx_all, 16)
                    pe.wait_ge(v_sb, NC)
                    cross_values(0)
                else:
                    features(g_bank[0], wqkv, 0, hT, q_ps)
                turn_probs(i, 2, started)
                values(i, 1, started)
                if not first:
                    if last:
                        pe.wait_ge(w_sb, i - 1)
                    else:
                        pe.wait_ge(k_sb, i + 2)
                    cross_turn(i - 1)
                turn_probs(i, 3, started)
                if not last:
                    pe.wait_ge(q_sb, i + 2)
                    tokens(both(g_bank[0]), hT, wqkv, D, 2 * D, v_ps)
                values(i, 2, started)
                values(i, 3, started)
                if not first:
                    pe.wait_ge(x1nT_lo, i)
                    pe.wait_ge(pT_sb, UNITS * (i + 1) - 1)
                    cross_queries(i - 1, t_bank[0])
                else:
                    pe.wait_ge(ld_const, 16)
                    pe.wait_ge(v_sb, 1)
                    for h in range(KT):
                        mm = pe.matmul(g_bank[1][:, h * P:(h + 1) * P], whT_sb[:, h, :], whT_sb[:, h, :],
                                       start=True, stop=True)
                    mm.then_inc(gram_ps, 1)
                if last:
                    pe.wait_ge(sub_sb, UNITS * (i + 1))
                for t in range(TPC):
                    pe.wait_ge(att_sb, TPC * i + t + 1)
                    for k in range(KT):
                        mm = pe.transpose((s_bank[1] if last else t_bank[1])[:, k * TOK + t * P:k * TOK + t * P + P],
                                          att[:, t, k * P:(k + 1) * P], ident)
                mm.then_inc(attT_ps, 1)
                if first:
                    pe.wait_ge(k_sb, 2)
                    stay_awake(4)
                else:
                    if not last:
                        cross_gate(i - 1, g_bank[1])
                        pe.wait_ge(qp_sb, i)
                if not last:
                    scores(i + 1, 0, True)
                    scores(i + 1, 1, True)
                if first:
                    pe.wait_ge(wag_lo, 1)
                    pe.wait_ge(gram_sb_done, 1)
                pe.wait_ge(attT_hi, i + 1)
                tokens(both(s_bank[0] if last else t_bank[0]), attT, wout, D, 0, y_ps, (attT_lo, i + 1))
                if last:
                    cross_gate(i - 1, g_bank[1])
                    cross_scores(i - 1, ctxT[:, :, :], ld_ctx)

            pe.wait_ge(zeros_set, 1)
            stay_awake(WAKE)
            pe.wait_ge(ld_first, 16)
            pe.wait_ge(hn_sb, TPC)
            turn(g_bank[0], hn, hT_ps)
            pe.wait_ge(wqkv_hi, 1)
            pe.wait_ge(wqkv_lo, 1)
            pe.wait_ge(hT_hi, 1)
            features(g_bank[1], wqkv, D, hT, k_ps, (hT_lo, 1))
            pe.wait_ge(wqkv_lo, 2)
            features(g_bank[0], wqkv, 0, hT, q_ps)
            pe.wait_ge(wqkv_lo, 3)
            pe.wait_ge(k_sb, 1)
            tokens(both(g_bank[1]), hT, wqkv, D, 2 * D, v_ps)
            pe.wait_ge(pool_const, 3)
            pe.wait_ge(ld_mask, 16)
            mask_product(c_bank).then_inc(mask_ps, 1)

            scores(0, 0, False)
            scores(0, 1, False)
            attention(0, True, False)
            pe.wait_ge(wag_lo, 2)
            pe.wait_ge(gram_lo, 1)
            attention(1, False, False)
            with pe.Fori(2, NC - 1) as i:
                attention(i, False, False)
            attention(NC - 1, False, True)
            cross_values(1)
            cross_values(2)
            pe.wait_ge(x1n_sb, TPC * NC)
            turn(t_bank[0], x1n, x1nT_ps)
            cross_values(3)
            pe.wait_ge(x1nT_hi, NC)
            cross_queries(NC - 1, s_bank[1])
            cross_values(4)
            cross_scores(NC - 1, v_all[:, NC - 1], None)
            pe.wait_ge(x1_sb, NC)
            cross_gate(NC - 1, s_bank[0])

            def cross_out(c, bank=o_bank):
                if type(c) is not int or c > 1:
                    pe.wait_ge(on_sb, TPC * (c - 1))
                for h in range(KT):
                    mm = pe.matmul(bank[:, :].rearrange("p (t h e) -> p t h e", t=TPC, h=KT)[:, :, h, :],
                                   aT[:, h, :], v_all[:, c, h, :], start=True, stop=True)
                mm.then_inc(o_ps, 1)

            def norm_turn(c):
                if type(c) is int and c == 0:
                    pe.wait_ge(on_sb, TPC)
                else:
                    pe.wait_ge(on_sb, TPC * c)
                    pe.wait_ge(yT_sb, KT * c)
                turn(t_bank[0], on, yT_ps)

            def second(j, head, tail, turns, more):
                if head:
                    pe.wait_ge(x2n0_sb, j)
                    pe.wait_ge(x2n1_sb, j)
                    if type(j) is not int or j > 1:
                        pe.wait_ge(x2nT_lo, j - 1)
                    turn(t_bank[1], x2n, x2nT_ps)
                if not tail and turns is None:
                    stay_awake(8)
                if tail:
                    pe.wait_ge(zT_hi, j + 1)
                    if type(j) is not int or j > 0:
                        pe.wait_ge(x2_sb, j)
                    tokens(both(g_bank[1]), zT, wo, D, 0, z_ps, (zT_lo, j + 1))
                if head:
                    pe.wait_ge(x2nT_hi, j)
                    if type(j) is not int or j > 1:
                        pe.wait_ge(uT_lo, j - 1)
                    features(s_bank[0], wup, 0, x2nT, up_ps, (x2nT_lo, j))
                if turns:
                    norm_turn(j + 1)
                if head:
                    if type(j) is not int or j > 1:
                        pe.wait_ge(moe_sb, TPC * (j - 1))
                    else:
                        pe.wait_ge(x2_sb, 2)
                    tokens([(bank, 0) for bank in EX_BANKS], x2nT, wex, D + E, 0, ex_ps)
                if more:
                    cross_out(j + 2)
                if head:
                    pe.wait_ge(uT_hi, j)
                    if type(j) is not int or 1 < j < NC - 2:
                        pe.wait_ge(dn_sb, j - 1)
                    elif j > NC - 2:
                        pe.wait_ge(dn_sb, j - 2)
                    tokens(both(down_bank(j - 1)), uT, wdn, D, 0, dn_ps, (uT_lo, j))

            pe.wait_ge(aT_sb, 1)
            pe.wait_ge(later_lo, STEPS)
            pe.wait_ge(vx_sb, 4)
            cross_out(0)
            cross_out(1, t_bank[1])
            cross_values(5)
            cross_values(6)
            pe.wait_ge(w_sb, NC - 1)
            cross_values(7)
            norm_turn(0)
            pe.wait_ge(on1_sb, TPC)
            pe.wait_ge(w_sb, NC)
            turn(s_bank[0], x2n, yT_ps)
            cross_out(2)
            stay_awake(6)
            pe.wait_ge(vx_sb, NC)
            pe.wait_ge(zT_hi, 1)
            tokens(both(g_bank[1]), zT, wo, D, 0, z_ps, (zT_lo, 1))
            pe.wait_ge(zT_hi, 2)
            tokens(both(s_bank[1]), uT, wo, D, 0, z_ps, (zT_lo, 2))
            norm_turn(2)
            cross_out(3)
            stay_awake(4)
            second(1, True, False, None, False)
            second(2, True, True, True, True)
            with pe.Fori(3, NC - 2) as j:
                second(j, True, True, True, True)
            second(NC - 2, True, True, True, False)
            second(NC - 1, True, True, False, False)
            second(NC, True, False, False, False)


def kernel(**inputs):
    import ml_dtypes
    import numpy as np
    import concourse.bacc as _bacc
    from concourse import mybir as _mybir
    from concourse.bass_utils import run_bass_kernel_spmd as _run

    a = {n: np.ascontiguousarray(v) for n, v in inputs.items()}
    b_qkv = a["L0_attn_b_qkv"]
    d = b_qkv.size // 3
    b, s = a["x"].shape[:2]
    kt = d // P
    tpc = 2

    window = 64
    mask = np.zeros((P, P + window), ml_dtypes.bfloat16)
    mask[np.arange(P) % window, np.arange(P)] = 1
    mask[:window, P:][np.triu_indices(window, 1)] = -1e30
    heads, hd = a["L0_xattn_Wh"].shape[:2]
    gam = (1.0 - 2.0 ** (-5.0 - np.arange(heads))).astype(np.float32)
    idx = np.arange(s, dtype=np.float32)
    expo = idx[None, :] - idx[:, None]
    dm = np.where(expo[None] <= 0, gam[:, None, None] ** expo[None], np.float32(0)).astype(np.float32)
    dm = dm / np.sqrt(dm.sum(axis=-1))[:, None, :]
    decay = (dm / np.sqrt(np.float32(hd))).transpose(2, 0, 1).reshape(P, -1).astype(np.float32)

    def by_half(w):
        return w.reshape(kt, P, -1).transpose(1, 0, 2).reshape(P, -1)

    def columns(v):
        return v.reshape(-1, P).T

    def rows(v):
        return np.broadcast_to(v, (P, v.size))

    wh = a["L0_xattn_Wh"]
    wex = np.concatenate([a["L0_ffn_W_expert"], a["L0_ffn_W_gate"].T], axis=1)
    arrays = {
        "x": a["x"],
        "ctx": a["ctx_2048"].reshape(b // tpc, tpc, s, kt, P).transpose(0, 4, 3, 1, 2).reshape(b // tpc, P, kt, tpc * s),
        "first": np.concatenate([np.eye(P, dtype=np.float32), columns(b_qkv[:2 * d]),
                                 np.repeat(np.eye(P // 16, dtype=np.float32), 16, axis=0)], axis=1),
        "w_qkv": a["L0_attn_W_qkv"],
        "const": np.concatenate([
            rows(b_qkv[2 * d:]), rows(a["L0_attn_b_out"]), decay,
            wh.transpose(1, 0, 2).reshape(P, -1), wh.transpose(2, 0, 1).reshape(P, -1),
            columns(a["L0_xattn_gn_gamma"]), columns(a["L0_xattn_gn_beta"])], axis=1),
        "weights": np.concatenate([by_half(w) for w in (
            a["L0_attn_W_out"], a["L0_xattn_wg_w"], a["L0_xattn_wo_w"], a["L0_ffn_W_up"].T, a["L0_ffn_W_down"].T,
            wex)], axis=1),
        "mask": mask,
    }
    arrays = {f"in_{n}_dram": np.ascontiguousarray(v) for n, v in arrays.items()}
    nc = _bacc.Bacc("TRN2", target_bir_lowering=False, num_devices=1)
    args = [nc.dram_tensor(n, v.shape, _mybir.dt.from_np(v.dtype), kind="ExternalInput").ap()
            for n, v in arrays.items()]
    args.append(nc.dram_tensor("out_0_dram", a["x"].shape, _mybir.dt.from_np(a["x"].dtype),
                               kind="ExternalOutput").ap())
    bass_decoder_layer_kernel(nc, *args)
    r = _run(nc, [arrays], core_ids=[0])
    return r.results[0]["out_0_dram"]
```
